# Optimizing a Trainium2 kernel written in Bass

```python
import numpy as np
import jax
import jax.numpy as jnp

def _softmax(x, axis=-1):
    return jax.nn.softmax(x, axis=axis)

def _gelu(x):
    return jax.nn.gelu(x, approximate=True)

def _silu(x):
    return jax.nn.silu(x)

def _sigmoid(x):
    return jax.nn.sigmoid(x)

def _layernorm(x, axis=-1, eps=1e-05):
    m = jnp.mean(x, axis=axis, keepdims=True)
    v = jnp.var(x, axis=axis, keepdims=True)
    return (x - m) / jnp.sqrt(v + eps)

def _scatter_add(tgt, idx, src, axis=0):
    return tgt.at[idx].add(src)

def _segment_sum(src, seg, n):
    return jax.ops.segment_sum(src, seg, n)
kernel_name = 'mk_rec_standalone_d1_rec_r8_c23496'

def setup_inputs(seed: int=0):
    np.random.seed(seed)
    _w = jnp.asarray

    def _rec_inputs():
        import jax
        import jax.numpy as jnp
        _rk = jax.random.key(seed)
        r_user_dense = 0.00708528 + 1.00131 * jax.random.normal(jax.random.fold_in(_rk, 1), (2048, 25), jnp.float32)
        r_user_id = jax.random.randint(jax.random.fold_in(_rk, 2), (2048,), 78, 199964, jnp.int32)
        r_item_id = jax.random.randint(jax.random.fold_in(_rk, 3), (2048,), 202, 499889, jnp.int32)
        r_item_category = jax.random.randint(jax.random.fold_in(_rk, 4), (2048,), 0, 999, jnp.int32)
        r_item_dur_bkt = jax.random.randint(jax.random.fold_in(_rk, 5), (2048,), 0, 20, jnp.int32)
        r_item_dense = -0.0146907 + 0.998195 * jax.random.normal(jax.random.fold_in(_rk, 6), (2048, 3), jnp.float32)
        r_history_seq = jnp.stack([jax.random.randint(jax.random.fold_in(jax.random.fold_in(_rk, 7), 0), (2048,), 1, 499901, jnp.int32), jax.random.randint(jax.random.fold_in(jax.random.fold_in(_rk, 7), 1), (2048,), 25, 499996, jnp.int32), jax.random.randint(jax.random.fold_in(jax.random.fold_in(_rk, 7), 2), (2048,), 107, 499691, jnp.int32), jax.random.randint(jax.random.fold_in(jax.random.fold_in(_rk, 7), 3), (2048,), 79, 499987, jnp.int32), jax.random.randint(jax.random.fold_in(jax.random.fold_in(_rk, 7), 4), (2048,), 147, 499988, jnp.int32), jax.random.randint(jax.random.fold_in(jax.random.fold_in(_rk, 7), 5), (2048,), 162, 499975, jnp.int32), jax.random.randint(jax.random.fold_in(jax.random.fold_in(_rk, 7), 6), (2048,), 12, 499903, jnp.int32), jax.random.randint(jax.random.fold_in(jax.random.fold_in(_rk, 7), 7), (2048,), 24, 62481, jnp.int32), jax.random.randint(jax.random.fold_in(jax.random.fold_in(_rk, 7), 8), (2048,), 202, 499826, jnp.int32), jax.random.randint(jax.random.fold_in(jax.random.fold_in(_rk, 7), 9), (2048,), 292, 499962, jnp.int32), jax.random.randint(jax.random.fold_in(jax.random.fold_in(_rk, 7), 10), (2048,), 86, 499927, jnp.int32), jax.random.randint(jax.random.fold_in(jax.random.fold_in(_rk, 7), 11), (2048,), 169, 499927, jnp.int32), jax.random.randint(jax.random.fold_in(jax.random.fold_in(_rk, 7), 12), (2048,), 200, 499925, jnp.int32), jax.random.randint(jax.random.fold_in(jax.random.fold_in(_rk, 7), 13), (2048,), 25, 499941, jnp.int32), jax.random.randint(jax.random.fold_in(jax.random.fold_in(_rk, 7), 14), (2048,), 6, 499886, jnp.int32), jax.random.randint(jax.random.fold_in(jax.random.fold_in(_rk, 7), 15), (2048,), 60, 499829, jnp.int32), jax.random.randint(jax.random.fold_in(jax.random.fold_in(_rk, 7), 16), (2048,), 101, 499979, jnp.int32), jax.random.randint(jax.random.fold_in(jax.random.fold_in(_rk, 7), 17), (2048,), 46, 499982, jnp.int32), jax.random.randint(jax.random.fold_in(jax.random.fold_in(_rk, 7), 18), (2048,), 88, 499983, jnp.int32), jax.random.randint(jax.random.fold_in(jax.random.fold_in(_rk, 7), 19), (2048,), 83, 499979, jnp.int32), jax.random.randint(jax.random.fold_in(jax.random.fold_in(_rk, 7), 20), (2048,), 60, 499934, jnp.int32), jax.random.randint(jax.random.fold_in(jax.random.fold_in(_rk, 7), 21), (2048,), 26, 62499, jnp.int32), jax.random.randint(jax.random.fold_in(jax.random.fold_in(_rk, 7), 22), (2048,), 216, 499958, jnp.int32), jax.random.randint(jax.random.fold_in(jax.random.fold_in(_rk, 7), 23), (2048,), 408, 499983, jnp.int32), jax.random.randint(jax.random.fold_in(jax.random.fold_in(_rk, 7), 24), (2048,), 7, 499855, jnp.int32), jax.random.randint(jax.random.fold_in(jax.random.fold_in(_rk, 7), 25), (2048,), 105, 499915, jnp.int32), jax.random.randint(jax.random.fold_in(jax.random.fold_in(_rk, 7), 26), (2048,), 239, 499924, jnp.int32), jax.random.randint(jax.random.fold_in(jax.random.fold_in(_rk, 7), 27), (2048,), 114, 499865, jnp.int32), jax.random.randint(jax.random.fold_in(jax.random.fold_in(_rk, 7), 28), (2048,), 252, 499581, jnp.int32), jax.random.randint(jax.random.fold_in(jax.random.fold_in(_rk, 7), 29), (2048,), 178, 499989, jnp.int32), jax.random.randint(jax.random.fold_in(jax.random.fold_in(_rk, 7), 30), (2048,), 246, 499589, jnp.int32), jax.random.randint(jax.random.fold_in(jax.random.fold_in(_rk, 7), 31), (2048,), 33, 62500, jnp.int32), jax.random.randint(jax.random.fold_in(jax.random.fold_in(_rk, 7), 32), (2048,), 154, 499967, jnp.int32), jax.random.randint(jax.random.fold_in(jax.random.fold_in(_rk, 7), 33), (2048,), 467, 499862, jnp.int32), jax.random.randint(jax.random.fold_in(jax.random.fold_in(_rk, 7), 34), (2048,), 135, 62492, jnp.int32), jax.random.randint(jax.random.fold_in(jax.random.fold_in(_rk, 7), 35), (2048,), 3, 62494, jnp.int32), jax.random.randint(jax.random.fold_in(jax.random.fold_in(_rk, 7), 36), (2048,), 57, 499793, jnp.int32), jax.random.randint(jax.random.fold_in(jax.random.fold_in(_rk, 7), 37), (2048,), 72, 62493, jnp.int32), jax.random.randint(jax.random.fold_in(jax.random.fold_in(_rk, 7), 38), (2048,), 88, 499836, jnp.int32), jax.random.randint(jax.random.fold_in(jax.random.fold_in(_rk, 7), 39), (2048,), 18, 499999, jnp.int32), jax.random.randint(jax.random.fold_in(jax.random.fold_in(_rk, 7), 40), (2048,), 300, 499694, jnp.int32), jax.random.randint(jax.random.fold_in(jax.random.fold_in(_rk, 7), 41), (2048,), 14, 499661, jnp.int32), jax.random.randint(jax.random.fold_in(jax.random.fold_in(_rk, 7), 42), (2048,), 31, 499803, jnp.int32), jax.random.randint(jax.random.fold_in(jax.random.fold_in(_rk, 7), 43), (2048,), 465, 62493, jnp.int32), jax.random.randint(jax.random.fold_in(jax.random.fold_in(_rk, 7), 44), (2048,), 48, 499980, jnp.int32), jax.random.randint(jax.random.fold_in(jax.random.fold_in(_rk, 7), 45), (2048,), 408, 499709, jnp.int32), jax.random.randint(jax.random.fold_in(jax.random.fold_in(_rk, 7), 46), (2048,), 130, 499865, jnp.int32), jax.random.randint(jax.random.fold_in(jax.random.fold_in(_rk, 7), 47), (2048,), 99, 62468, jnp.int32), jax.random.randint(jax.random.fold_in(jax.random.fold_in(_rk, 7), 48), (2048,), 119, 499588, jnp.int32), jax.random.randint(jax.random.fold_in(jax.random.fold_in(_rk, 7), 49), (2048,), 634, 499993, jnp.int32), jax.random.randint(jax.random.fold_in(jax.random.fold_in(_rk, 7), 50), (2048,), 363, 499807, jnp.int32), jax.random.randint(jax.random.fold_in(jax.random.fold_in(_rk, 7), 51), (2048,), 45, 499859, jnp.int32), jax.random.randint(jax.random.fold_in(jax.random.fold_in(_rk, 7), 52), (2048,), 95, 499923, jnp.int32), jax.random.randint(jax.random.fold_in(jax.random.fold_in(_rk, 7), 53), (2048,), 160, 499715, jnp.int32), jax.random.randint(jax.random.fold_in(jax.random.fold_in(_rk, 7), 54), (2048,), 295, 499985, jnp.int32), jax.random.randint(jax.random.fold_in(jax.random.fold_in(_rk, 7), 55), (2048,), 544, 499998, jnp.int32), jax.random.randint(jax.random.fold_in(jax.random.fold_in(_rk, 7), 56), (2048,), 351, 499933, jnp.int32), jax.random.randint(jax.random.fold_in(jax.random.fold_in(_rk, 7), 57), (2048,), 128, 62486, jnp.int32), jax.random.randint(jax.random.fold_in(jax.random.fold_in(_rk, 7), 58), (2048,), 155, 499986, jnp.int32), jax.random.randint(jax.random.fold_in(jax.random.fold_in(_rk, 7), 59), (2048,), 433, 499591, jnp.int32), jax.random.randint(jax.random.fold_in(jax.random.fold_in(_rk, 7), 60), (2048,), 260, 499990, jnp.int32), jax.random.randint(jax.random.fold_in(jax.random.fold_in(_rk, 7), 61), (2048,), 23, 499887, jnp.int32), jax.random.randint(jax.random.fold_in(jax.random.fold_in(_rk, 7), 62), (2048,), 113, 499519, jnp.int32), jax.random.randint(jax.random.fold_in(jax.random.fold_in(_rk, 7), 63), (2048,), 162, 499956, jnp.int32), jax.random.randint(jax.random.fold_in(jax.random.fold_in(_rk, 7), 64), (2048,), 20, 499900, jnp.int32), jax.random.randint(jax.random.fold_in(jax.random.fold_in(_rk, 7), 65), (2048,), 171, 499915, jnp.int32), jax.random.randint(jax.random.fold_in(jax.random.fold_in(_rk, 7), 66), (2048,), 44, 62463, jnp.int32), jax.random.randint(jax.random.fold_in(jax.random.fold_in(_rk, 7), 67), (2048,), 33, 499742, jnp.int32), jax.random.randint(jax.random.fold_in(jax.random.fold_in(_rk, 7), 68), (2048,), 147, 499844, jnp.int32), jax.random.randint(jax.random.fold_in(jax.random.fold_in(_rk, 7), 69), (2048,), 14, 62469, jnp.int32), jax.random.randint(jax.random.fold_in(jax.random.fold_in(_rk, 7), 70), (2048,), 30, 499679, jnp.int32), jax.random.randint(jax.random.fold_in(jax.random.fold_in(_rk, 7), 71), (2048,), 108, 499986, jnp.int32), jax.random.randint(jax.random.fold_in(jax.random.fold_in(_rk, 7), 72), (2048,), 31, 499805, jnp.int32), jax.random.randint(jax.random.fold_in(jax.random.fold_in(_rk, 7), 73), (2048,), 188, 499838, jnp.int32), jax.random.randint(jax.random.fold_in(jax.random.fold_in(_rk, 7), 74), (2048,), 200, 499829, jnp.int32), jax.random.randint(jax.random.fold_in(jax.random.fold_in(_rk, 7), 75), (2048,), 86, 499925, jnp.int32), jax.random.randint(jax.random.fold_in(jax.random.fold_in(_rk, 7), 76), (2048,), 30, 62497, jnp.int32), jax.random.randint(jax.random.fold_in(jax.random.fold_in(_rk, 7), 77), (2048,), 5, 499994, jnp.int32), jax.random.randint(jax.random.fold_in(jax.random.fold_in(_rk, 7), 78), (2048,), 157, 62489, jnp.int32), jax.random.randint(jax.random.fold_in(jax.random.fold_in(_rk, 7), 79), (2048,), 308, 499949, jnp.int32), jax.random.randint(jax.random.fold_in(jax.random.fold_in(_rk, 7), 80), (2048,), 224, 499994, jnp.int32), jax.random.randint(jax.random.fold_in(jax.random.fold_in(_rk, 7), 81), (2048,), 129, 499759, jnp.int32), jax.random.randint(jax.random.fold_in(jax.random.fold_in(_rk, 7), 82), (2048,), 139, 499812, jnp.int32), jax.random.randint(jax.random.fold_in(jax.random.fold_in(_rk, 7), 83), (2048,), 43, 499980, jnp.int32), jax.random.randint(jax.random.fold_in(jax.random.fold_in(_rk, 7), 84), (2048,), 368, 499775, jnp.int32), jax.random.randint(jax.random.fold_in(jax.random.fold_in(_rk, 7), 85), (2048,), 89, 499985, jnp.int32), jax.random.randint(jax.random.fold_in(jax.random.fold_in(_rk, 7), 86), (2048,), 64, 499926, jnp.int32), jax.random.randint(jax.random.fold_in(jax.random.fold_in(_rk, 7), 87), (2048,), 135, 62476, jnp.int32), jax.random.randint(jax.random.fold_in(jax.random.fold_in(_rk, 7), 88), (2048,), 57, 499871, jnp.int32), jax.random.randint(jax.random.fold_in(jax.random.fold_in(_rk, 7), 89), (2048,), 97, 62495, jnp.int32), jax.random.randint(jax.random.fold_in(jax.random.fold_in(_rk, 7), 90), (2048,), 393, 499977, jnp.int32), jax.random.randint(jax.random.fold_in(jax.random.fold_in(_rk, 7), 91), (2048,), 0, 499853, jnp.int32), jax.random.randint(jax.random.fold_in(jax.random.fold_in(_rk, 7), 92), (2048,), 4, 499956, jnp.int32), jax.random.randint(jax.random.fold_in(jax.random.fold_in(_rk, 7), 93), (2048,), 88, 499917, jnp.int32), jax.random.randint(jax.random.fold_in(jax.random.fold_in(_rk, 7), 94), (2048,), 102, 62481, jnp.int32), jax.random.randint(jax.random.fold_in(jax.random.fold_in(_rk, 7), 95), (2048,), 27, 500001, jnp.int32), jax.random.randint(jax.random.fold_in(jax.random.fold_in(_rk, 7), 96), (2048,), 61, 499998, jnp.int32), jax.random.randint(jax.random.fold_in(jax.random.fold_in(_rk, 7), 97), (2048,), 173, 499967, jnp.int32), jax.random.randint(jax.random.fold_in(jax.random.fold_in(_rk, 7), 98), (2048,), 113, 499814, jnp.int32), jax.random.randint(jax.random.fold_in(jax.random.fold_in(_rk, 7), 99), (2048,), 77, 499997, jnp.int32), jax.random.randint(jax.random.fold_in(jax.random.fold_in(_rk, 7), 100), (2048,), 4, 499999, jnp.int32), jax.random.randint(jax.random.fold_in(jax.random.fold_in(_rk, 7), 101), (2048,), 18, 499543, jnp.int32), jax.random.randint(jax.random.fold_in(jax.random.fold_in(_rk, 7), 102), (2048,), 57, 499971, jnp.int32), jax.random.randint(jax.random.fold_in(jax.random.fold_in(_rk, 7), 103), (2048,), 574, 499985, jnp.int32), jax.random.randint(jax.random.fold_in(jax.random.fold_in(_rk, 7), 104), (2048,), 78, 499991, jnp.int32), jax.random.randint(jax.random.fold_in(jax.random.fold_in(_rk, 7), 105), (2048,), 21, 499941, jnp.int32), jax.random.randint(jax.random.fold_in(jax.random.fold_in(_rk, 7), 106), (2048,), 121, 499991, jnp.int32), jax.random.randint(jax.random.fold_in(jax.random.fold_in(_rk, 7), 107), (2048,), 13, 499942, jnp.int32), jax.random.randint(jax.random.fold_in(jax.random.fold_in(_rk, 7), 108), (2048,), 39, 499961, jnp.int32), jax.random.randint(jax.random.fold_in(jax.random.fold_in(_rk, 7), 109), (2048,), 220, 62489, jnp.int32), jax.random.randint(jax.random.fold_in(jax.random.fold_in(_rk, 7), 110), (2048,), 401, 499998, jnp.int32), jax.random.randint(jax.random.fold_in(jax.random.fold_in(_rk, 7), 111), (2048,), 119, 499942, jnp.int32), jax.random.randint(jax.random.fold_in(jax.random.fold_in(_rk, 7), 112), (2048,), 24, 499922, jnp.int32), jax.random.randint(jax.random.fold_in(jax.random.fold_in(_rk, 7), 113), (2048,), 238, 499965, jnp.int32), jax.random.randint(jax.random.fold_in(jax.random.fold_in(_rk, 7), 114), (2048,), 240, 499956, jnp.int32), jax.random.randint(jax.random.fold_in(jax.random.fold_in(_rk, 7), 115), (2048,), 112, 499905, jnp.int32), jax.random.randint(jax.random.fold_in(jax.random.fold_in(_rk, 7), 116), (2048,), 11, 499973, jnp.int32), jax.random.randint(jax.random.fold_in(jax.random.fold_in(_rk, 7), 117), (2048,), 55, 499996, jnp.int32), jax.random.randint(jax.random.fold_in(jax.random.fold_in(_rk, 7), 118), (2048,), 60, 499926, jnp.int32), jax.random.randint(jax.random.fold_in(jax.random.fold_in(_rk, 7), 119), (2048,), 499, 499993, jnp.int32), jax.random.randint(jax.random.fold_in(jax.random.fold_in(_rk, 7), 120), (2048,), 316, 499916, jnp.int32), jax.random.randint(jax.random.fold_in(jax.random.fold_in(_rk, 7), 121), (2048,), 139, 62482, jnp.int32), jax.random.randint(jax.random.fold_in(jax.random.fold_in(_rk, 7), 122), (2048,), 39, 499570, jnp.int32), jax.random.randint(jax.random.fold_in(jax.random.fold_in(_rk, 7), 123), (2048,), 23, 499913, jnp.int32), jax.random.randint(jax.random.fold_in(jax.random.fold_in(_rk, 7), 124), (2048,), 120, 499918, jnp.int32), jax.random.randint(jax.random.fold_in(jax.random.fold_in(_rk, 7), 125), (2048,), 65, 499751, jnp.int32), jax.random.randint(jax.random.fold_in(jax.random.fold_in(_rk, 7), 126), (2048,), 166, 499877, jnp.int32), jax.random.randint(jax.random.fold_in(jax.random.fold_in(_rk, 7), 127), (2048,), 42, 62443, jnp.int32), jax.random.randint(jax.random.fold_in(jax.random.fold_in(_rk, 7), 128), (2048,), 72, 499786, jnp.int32), jax.random.randint(jax.random.fold_in(jax.random.fold_in(_rk, 7), 129), (2048,), 240, 499727, jnp.int32), jax.random.randint(jax.random.fold_in(jax.random.fold_in(_rk, 7), 130), (2048,), 37, 499863, jnp.int32), jax.random.randint(jax.random.fold_in(jax.random.fold_in(_rk, 7), 131), (2048,), 45, 499979, jnp.int32), jax.random.randint(jax.random.fold_in(jax.random.fold_in(_rk, 7), 132), (2048,), 77, 499961, jnp.int32), jax.random.randint(jax.random.fold_in(jax.random.fold_in(_rk, 7), 133), (2048,), 45, 62491, jnp.int32), jax.random.randint(jax.random.fold_in(jax.random.fold_in(_rk, 7), 134), (2048,), 180, 499997, jnp.int32), jax.random.randint(jax.random.fold_in(jax.random.fold_in(_rk, 7), 135), (2048,), 44, 499839, jnp.int32), jax.random.randint(jax.random.fold_in(jax.random.fold_in(_rk, 7), 136), (2048,), 204, 499989, jnp.int32), jax.random.randint(jax.random.fold_in(jax.random.fold_in(_rk, 7), 137), (2048,), 123, 499994, jnp.int32), jax.random.randint(jax.random.fold_in(jax.random.fold_in(_rk, 7), 138), (2048,), 116, 499982, jnp.int32), jax.random.randint(jax.random.fold_in(jax.random.fold_in(_rk, 7), 139), (2048,), 4, 499796, jnp.int32), jax.random.randint(jax.random.fold_in(jax.random.fold_in(_rk, 7), 140), (2048,), 18, 499818, jnp.int32), jax.random.randint(jax.random.fold_in(jax.random.fold_in(_rk, 7), 141), (2048,), 49, 499747, jnp.int32), jax.random.randint(jax.random.fold_in(jax.random.fold_in(_rk, 7), 142), (2048,), 78, 62499, jnp.int32), jax.random.randint(jax.random.fold_in(jax.random.fold_in(_rk, 7), 143), (2048,), 9, 499887, jnp.int32), jax.random.randint(jax.random.fold_in(jax.random.fold_in(_rk, 7), 144), (2048,), 10, 499837, jnp.int32), jax.random.randint(jax.random.fold_in(jax.random.fold_in(_rk, 7), 145), (2048,), 44, 499718, jnp.int32), jax.random.randint(jax.random.fold_in(jax.random.fold_in(_rk, 7), 146), (2048,), 46, 499790, jnp.int32), jax.random.randint(jax.random.fold_in(jax.random.fold_in(_rk, 7), 147), (2048,), 102, 499860, jnp.int32), jax.random.randint(jax.random.fold_in(jax.random.fold_in(_rk, 7), 148), (2048,), 56, 499949, jnp.int32), jax.random.randint(jax.random.fold_in(jax.random.fold_in(_rk, 7), 149), (2048,), 102, 499943, jnp.int32), jax.random.randint(jax.random.fold_in(jax.random.fold_in(_rk, 7), 150), (2048,), 173, 499975, jnp.int32), jax.random.randint(jax.random.fold_in(jax.random.fold_in(_rk, 7), 151), (2048,), 58, 499861, jnp.int32), jax.random.randint(jax.random.fold_in(jax.random.fold_in(_rk, 7), 152), (2048,), 404, 499933, jnp.int32), jax.random.randint(jax.random.fold_in(jax.random.fold_in(_rk, 7), 153), (2048,), 372, 499907, jnp.int32), jax.random.randint(jax.random.fold_in(jax.random.fold_in(_rk, 7), 154), (2048,), 112, 499934, jnp.int32), jax.random.randint(jax.random.fold_in(jax.random.fold_in(_rk, 7), 155), (2048,), 190, 499588, jnp.int32), jax.random.randint(jax.random.fold_in(jax.random.fold_in(_rk, 7), 156), (2048,), 122, 499690, jnp.int32), jax.random.randint(jax.random.fold_in(jax.random.fold_in(_rk, 7), 157), (2048,), 195, 499833, jnp.int32), jax.random.randint(jax.random.fold_in(jax.random.fold_in(_rk, 7), 158), (2048,), 36, 499778, jnp.int32), jax.random.randint(jax.random.fold_in(jax.random.fold_in(_rk, 7), 159), (2048,), 183, 499773, jnp.int32), jax.random.randint(jax.random.fold_in(jax.random.fold_in(_rk, 7), 160), (2048,), 137, 499858, jnp.int32), jax.random.randint(jax.random.fold_in(jax.random.fold_in(_rk, 7), 161), (2048,), 350, 499946, jnp.int32), jax.random.randint(jax.random.fold_in(jax.random.fold_in(_rk, 7), 162), (2048,), 50, 499969, jnp.int32), jax.random.randint(jax.random.fold_in(jax.random.fold_in(_rk, 7), 163), (2048,), 130, 62481, jnp.int32), jax.random.randint(jax.random.fold_in(jax.random.fold_in(_rk, 7), 164), (2048,), 35, 62491, jnp.int32), jax.random.randint(jax.random.fold_in(jax.random.fold_in(_rk, 7), 165), (2048,), 178, 499753, jnp.int32), jax.random.randint(jax.random.fold_in(jax.random.fold_in(_rk, 7), 166), (2048,), 42, 499805, jnp.int32), jax.random.randint(jax.random.fold_in(jax.random.fold_in(_rk, 7), 167), (2048,), 72, 499809, jnp.int32), jax.random.randint(jax.random.fold_in(jax.random.fold_in(_rk, 7), 168), (2048,), 24, 499902, jnp.int32), jax.random.randint(jax.random.fold_in(jax.random.fold_in(_rk, 7), 169), (2048,), 49, 499991, jnp.int32), jax.random.randint(jax.random.fold_in(jax.random.fold_in(_rk, 7), 170), (2048,), 10, 62447, jnp.int32), jax.random.randint(jax.random.fold_in(jax.random.fold_in(_rk, 7), 171), (2048,), 55, 499979, jnp.int32), jax.random.randint(jax.random.fold_in(jax.random.fold_in(_rk, 7), 172), (2048,), 272, 499465, jnp.int32), jax.random.randint(jax.random.fold_in(jax.random.fold_in(_rk, 7), 173), (2048,), 84, 499923, jnp.int32), jax.random.randint(jax.random.fold_in(jax.random.fold_in(_rk, 7), 174), (2048,), 20, 499923, jnp.int32), jax.random.randint(jax.random.fold_in(jax.random.fold_in(_rk, 7), 175), (2048,), 15, 62499, jnp.int32), jax.random.randint(jax.random.fold_in(jax.random.fold_in(_rk, 7), 176), (2048,), 446, 499994, jnp.int32), jax.random.randint(jax.random.fold_in(jax.random.fold_in(_rk, 7), 177), (2048,), 261, 499995, jnp.int32), jax.random.randint(jax.random.fold_in(jax.random.fold_in(_rk, 7), 178), (2048,), 50, 499947, jnp.int32), jax.random.randint(jax.random.fold_in(jax.random.fold_in(_rk, 7), 179), (2048,), 315, 499732, jnp.int32), jax.random.randint(jax.random.fold_in(jax.random.fold_in(_rk, 7), 180), (2048,), 85, 499841, jnp.int32), jax.random.randint(jax.random.fold_in(jax.random.fold_in(_rk, 7), 181), (2048,), 78, 499982, jnp.int32), jax.random.randint(jax.random.fold_in(jax.random.fold_in(_rk, 7), 182), (2048,), 33, 499990, jnp.int32), jax.random.randint(jax.random.fold_in(jax.random.fold_in(_rk, 7), 183), (2048,), 127, 499958, jnp.int32), jax.random.randint(jax.random.fold_in(jax.random.fold_in(_rk, 7), 184), (2048,), 377, 499967, jnp.int32), jax.random.randint(jax.random.fold_in(jax.random.fold_in(_rk, 7), 185), (2048,), 81, 499885, jnp.int32), jax.random.randint(jax.random.fold_in(jax.random.fold_in(_rk, 7), 186), (2048,), 52, 499983, jnp.int32), jax.random.randint(jax.random.fold_in(jax.random.fold_in(_rk, 7), 187), (2048,), 17, 499982, jnp.int32), jax.random.randint(jax.random.fold_in(jax.random.fold_in(_rk, 7), 188), (2048,), 90, 499989, jnp.int32), jax.random.randint(jax.random.fold_in(jax.random.fold_in(_rk, 7), 189), (2048,), 172, 499973, jnp.int32), jax.random.randint(jax.random.fold_in(jax.random.fold_in(_rk, 7), 190), (2048,), 4, 499981, jnp.int32), jax.random.randint(jax.random.fold_in(jax.random.fold_in(_rk, 7), 191), (2048,), 137, 499884, jnp.int32), jax.random.randint(jax.random.fold_in(jax.random.fold_in(_rk, 7), 192), (2048,), 235, 499926, jnp.int32), jax.random.randint(jax.random.fold_in(jax.random.fold_in(_rk, 7), 193), (2048,), 81, 499919, jnp.int32), jax.random.randint(jax.random.fold_in(jax.random.fold_in(_rk, 7), 194), (2048,), 375, 62476, jnp.int32), jax.random.randint(jax.random.fold_in(jax.random.fold_in(_rk, 7), 195), (2048,), 76, 499994, jnp.int32), jax.random.randint(jax.random.fold_in(jax.random.fold_in(_rk, 7), 196), (2048,), 114, 499833, jnp.int32), jax.random.randint(jax.random.fold_in(jax.random.fold_in(_rk, 7), 197), (2048,), 611, 499981, jnp.int32), jax.random.randint(jax.random.fold_in(jax.random.fold_in(_rk, 7), 198), (2048,), 464, 499747, jnp.int32), jax.random.randint(jax.random.fold_in(jax.random.fold_in(_rk, 7), 199), (2048,), 31, 499615, jnp.int32)], axis=1)
        return (r_user_dense, r_user_id, r_item_id, r_item_category, r_item_dur_bkt, r_item_dense, r_history_seq)
    r_user_dense, r_user_id, r_item_id, r_item_category, r_item_dur_bkt, r_item_dense, r_history_seq = _rec_inputs()

    def _L0_rec_setup():
        import jax, jax.numpy as jnp
        import numpy as np
        B, L = (512, 200)
        N_USERS, N_ITEMS, N_CATS, N_DUR = (25000, 62500, 1000, 20)
        D = 64

        def _lin(k, din, dout):
            kw, kb = jax.random.split(k)
            s = 1.0 / np.sqrt(din)
            return (jax.random.uniform(kw, (din, dout), minval=-s, maxval=s), jax.random.uniform(kb, (dout,), minval=-s, maxval=s))
        key = jax.random.key(seed)
        ks = jax.random.split(key, 20)
        inp = {'user_id': jax.random.randint(ks[0], (B,), 0, N_USERS), 'item_id': jax.random.randint(ks[1], (B,), 0, N_ITEMS), 'item_category': jax.random.randint(ks[2], (B,), 0, N_CATS), 'item_dur_bkt': jax.random.randint(ks[3], (B,), 0, N_DUR), 'user_dense': jax.random.normal(ks[4], (B, 25), dtype=jnp.float32), 'item_dense': jax.random.normal(ks[5], (B, 3), dtype=jnp.float32), 'history_seq': jax.random.randint(ks[6], (B, L), 0, N_ITEMS + 1), 'user_W': 0.01 * jax.random.normal(ks[7], (N_USERS, 64), dtype=jnp.float32), 'item_W': 0.01 * jax.random.normal(ks[8], (N_ITEMS, D), dtype=jnp.float32), 'cat_W': 0.01 * jax.random.normal(ks[9], (N_CATS, 16), dtype=jnp.float32), 'dur_W': 0.01 * jax.random.normal(ks[10], (N_DUR, 8), dtype=jnp.float32), 'hist_W': 0.01 * jax.random.normal(ks[11], (N_ITEMS + 1, D), dtype=jnp.float32)}
        inp['aW0'], inp['ab0'] = _lin(ks[12], 4 * D, 64)
        inp['aW1'], inp['ab1'] = _lin(ks[13], 64, 32)
        inp['aW2'], inp['ab2'] = _lin(ks[14], 32, 1)
        inp['mW0'], inp['mb0'] = _lin(ks[15], 244, 256)
        inp['mW1'], inp['mb1'] = _lin(ks[16], 256, 128)
        inp['mW2'], inp['mb2'] = _lin(ks[17], 128, 1)
        return inp
    _L0_rec_all = _L0_rec_setup()
    _L0_rec_in = {k: v for k, v in _L0_rec_all.items() if k in ('user_W', 'item_W', 'cat_W', 'dur_W', 'hist_W', 'aW0', 'ab0', 'aW1', 'ab1', 'aW2', 'ab2', 'mW0', 'mb0', 'mW1', 'mb1', 'mW2', 'mb2')}
    del _L0_rec_all
    return {'r_user_dense': r_user_dense, 'r_user_id': r_user_id, 'r_item_id': r_item_id, 'r_item_category': r_item_category, 'r_item_dur_bkt': r_item_dur_bkt, 'r_item_dense': r_item_dense, 'r_history_seq': r_history_seq, 'L0_rec_user_W': _L0_rec_in['user_W'], 'L0_rec_item_W': _L0_rec_in['item_W'], 'L0_rec_cat_W': _L0_rec_in['cat_W'], 'L0_rec_dur_W': _L0_rec_in['dur_W'], 'L0_rec_hist_W': _L0_rec_in['hist_W'], 'L0_rec_aW0': _L0_rec_in['aW0'], 'L0_rec_ab0': _L0_rec_in['ab0'], 'L0_rec_aW1': _L0_rec_in['aW1'], 'L0_rec_ab1': _L0_rec_in['ab1'], 'L0_rec_aW2': _L0_rec_in['aW2'], 'L0_rec_ab2': _L0_rec_in['ab2'], 'L0_rec_mW0': _L0_rec_in['mW0'], 'L0_rec_mb0': _L0_rec_in['mb0'], 'L0_rec_mW1': _L0_rec_in['mW1'], 'L0_rec_mb1': _L0_rec_in['mb1'], 'L0_rec_mW2': _L0_rec_in['mW2'], 'L0_rec_mb2': _L0_rec_in['mb2']}

def reference(r_user_dense, r_user_id, r_item_id, r_item_category, r_item_dur_bkt, r_item_dense, r_history_seq, L0_rec_user_W, L0_rec_item_W, L0_rec_cat_W, L0_rec_dur_W, L0_rec_hist_W, L0_rec_aW0, L0_rec_ab0, L0_rec_aW1, L0_rec_ab1, L0_rec_aW2, L0_rec_ab2, L0_rec_mW0, L0_rec_mb0, L0_rec_mW1, L0_rec_mb1, L0_rec_mW2, L0_rec_mb2):
    import jax
    import jax.numpy as jnp

    def _L0_rec_ref(user_id, item_id, item_category, item_dur_bkt, user_dense, item_dense, history_seq, user_W, item_W, cat_W, dur_W, hist_W, aW0, ab0, aW1, ab1, aW2, ab2, mW0, mb0, mW1, mb1, mW2, mb2):
        import jax, jax.numpy as jnp
        import numpy as np
        B, L = (512, 200)
        N_USERS, N_ITEMS, N_CATS, N_DUR = (25000, 62500, 1000, 20)
        D = 64

        def _lin(k, din, dout):
            kw, kb = jax.random.split(k)
            s = 1.0 / np.sqrt(din)
            return (jax.random.uniform(kw, (din, dout), minval=-s, maxval=s), jax.random.uniform(kb, (dout,), minval=-s, maxval=s))
        u_emb = user_W[user_id]
        i_emb = item_W[item_id]
        c_emb = cat_W[item_category]
        d_emb = dur_W[item_dur_bkt]
        hist = hist_W[history_seq]
        t = i_emb[:, None, :]
        tb = jnp.broadcast_to(t, hist.shape)
        feat = jnp.concatenate([hist, tb, hist * t, hist - t], axis=-1)
        h = jax.nn.relu(feat @ aW0 + ab0)
        h = jax.nn.relu(h @ aW1 + ab1)
        scores = (h @ aW2 + ab2)[..., 0]
        pad_mask = history_seq == 0
        scores = jnp.where(pad_mask, jnp.float32(-1000000000.0), scores)
        w = jax.nn.softmax(scores, axis=-1)
        pooled = jnp.einsum('bl,bld->bd', w, hist)
        x = jnp.concatenate([u_emb, i_emb, c_emb, d_emb, user_dense, item_dense, pooled], axis=-1)
        h = jax.nn.relu(x @ mW0 + mb0)
        h = jax.nn.relu(h @ mW1 + mb1)
        logit = (h @ mW2 + mb2)[..., 0]
        return jax.nn.sigmoid(logit)
    y = _L0_rec_ref(r_user_id, r_item_id, r_item_category, r_item_dur_bkt, r_user_dense, r_item_dense, r_history_seq, L0_rec_user_W, L0_rec_item_W, L0_rec_cat_W, L0_rec_dur_W, L0_rec_hist_W, L0_rec_aW0, L0_rec_ab0, L0_rec_aW1, L0_rec_ab1, L0_rec_aW2, L0_rec_ab2, L0_rec_mW0, L0_rec_mb0, L0_rec_mW1, L0_rec_mb1, L0_rec_mW2, L0_rec_mb2)
    return y

_drawn_inputs = setup_inputs


def setup_inputs(seed=0):
    import zlib

    import numpy as np

    out = dict(_drawn_inputs(seed))
    spreads = {}
    factors = {'r_user_dense': 4.483,
     'r_item_dense': 8.0,
     'L0_rec_user_W': 8.0,
     'L0_rec_item_W': 8.0,
     'L0_rec_cat_W': 23.596,
     'L0_rec_dur_W': 32.413,
     'L0_rec_hist_W': 24.839,
     'L0_rec_aW0': 22.173,
     'L0_rec_ab0': 64.0,
     'L0_rec_aW1': 8.0,
     'L0_rec_ab1': 200.0,
     'L0_rec_aW2': 26.266,
     'L0_rec_mW0': 4.014,
     'L0_rec_mb0': 8.0,
     'L0_rec_mW1': 3.939,
     'L0_rec_mb1': 4.655,
     'L0_rec_mW2': 4.709}
    for name, (base, spread) in spreads.items():
        noise = np.random.default_rng([zlib.crc32(name.encode()), seed]).standard_normal(out[name].shape)
        drawn = base * np.exp(spread * noise) if base else spread * noise
        out[name] = jnp.asarray(drawn.astype(out[name].dtype))
    for name, factor in factors.items():
        out[name] = (out[name] * factor).astype(out[name].dtype)
    return out
```

```python
from contextlib import ExitStack

import concourse.bass as bass
from concourse import mybir

F32 = mybir.dt.float32
I32 = mybir.dt.int32
ALU = mybir.AluOpType
ACT = mybir.ActivationFunctionType
AX = mybir.AxisListType

P = 128
SLOTS = 8
PAIRS = SLOTS // 2
MASKED = -1.0e9
ABSENT = -3.0e9
TAKEN = -3.0e38


def build(nc, a, out):
    B, L = a["history"].shape
    LAST = a["hist_W"].shape[0] - 1
    D = a["hist_W"].shape[1]
    G = B // P
    MAXC = L // SLOTS
    DUMMY = 4
    NK = (G * MAXC + MAXC) * SLOTS
    NU, NI = a["user_W"].shape[0], a["item_W"].shape[0]
    NC_, DC = a["cat_W"].shape
    ND, DD = a["dur_W"].shape
    H1, H2 = a["aW1"].shape
    FU, FI = a["user_dense"].shape[1], a["item_dense"].shape[1]
    M0, M1 = a["mW1"].shape
    X_USER, X_ITEM, X_CAT = 0, D, 2 * D
    X_DUR = X_CAT + DC
    X_UD = X_DUR + DD
    X_ID = X_UD + FU
    X_POOL = X_ID + FI
    XW = X_POOL + D
    XB = XW - P
    N = PAIRS * P
    AW = D + 1
    assert B % P == 0 and L % SLOTS == 0 and 2 * D == P and 4 * H2 == P and M0 == 2 * P and M1 == P

    ctx = ExitStack()
    with ctx:
        def sb(name, shape, dt=F32):
            return ctx.enter_context(nc.sbuf_tensor(name, shape, dt))

        def psum(name, shape):
            return ctx.enter_context(nc.psum_tensor(name, shape, F32))

        def sem(name):
            return ctx.enter_context(nc.semaphore(name))

        hist_ids = sb("hist_ids", [P, G + 1, L], I32)
        raw_ids = sb("raw_ids", [P, 4, G], I32)
        row_ids = sb("row_ids", [P, 4, G], I32)
        wrap_ids = sb("wrap_ids", [P, 4, G])
        in_range = sb("in_range", [P, G, L])
        row_count = sb("row_count", [P, G])
        max_col = sb("max_col", [G, 1])
        chunks_i = sb("chunks_i", [G, 1], I32)
        chunks_i2 = sb("chunks_i2", [G, 1], I32)
        chunks_f = sb("chunks_f", [G, 1])
        plan = sb("plan", [1, 64], I32)
        ident = sb("ident", [P, P])
        scan = sb("scan", [G, 2 * G + 1])
        key = sb("key", [P, L])
        key_wrap = sb("key_wrap", [P, L])
        key_neg = sb("key_neg", [P, L])
        top8 = sb("top8", [P, SLOTS])
        top8_row = sb("top8_row", [P, SLOTS])
        rows_all = sb("rows_all", [P, NK], I32)
        vals_all = sb("vals_all", [P, NK])
        keep_all = sb("keep_all", [P, NK])
        pen_all = sb("pen_all", [P, NK])
        pen_pad = sb("pen_pad", [P, L])
        n_real = sb("n_real", [P, 1])
        n_last = sb("n_last", [P, G + 1])
        has_last = sb("has_last", [P, 1])
        has_pen = sb("has_pen", [P, 1])
        last_kept = sb("last_kept", [P, 1])
        last_start = sb("last_start", [P, G + 1])
        last_score = sb("last_score", [P, G + 1])
        idx = [sb(f"idx{p}", [P, SLOTS], I32) for p in range(2)]
        hist_in = sb("hist_in", [P, 2, SLOTS, D])
        hist_pe = sb("hist_pe", [P, SLOTS * D])
        rows_x = sb("rows_x", [P, 2, SLOTS + 1, AW])
        hT = sb("hT", [P, N])
        pT = sb("pT", [P, N])
        h1 = sb("h1", [P, N])
        h2 = sb("h2", [P, N // 2])
        score9 = sb("score9", [P, SLOTS + 1])
        neg_max = sb("neg_max", [P, 1])
        e9 = sb("e9", [P, SLOTS + 1])
        prod = sb("prod", [P, SLOTS + 1, AW])
        inv_sum = sb("inv_sum", [P, 1])
        itemT = sb("itemT", [P, G * P])
        x_all = sb("x_all", [P, G + 1, XW])
        x_pe = sb("x_pe", [P, XW])
        xT = sb("xT", [P, 2 * P])
        m0 = sb("m0", [P, 2 * P])
        m1 = sb("m1", [P, P])
        logits = sb("logits", [P, G + 1])
        probs = sb("probs", [P, G])
        w_hist = sb("w_hist", [P, P])
        w_diff = sb("w_diff", [P, P])
        w_prod = sb("w_prod", [P, P])
        w_item = sb("w_item", [P, P])
        w_last = sb("w_last", [D, H1])
        w_tmp = sb("w_tmp", [D, H1])
        w_diff_lo = sb("w_diff_lo", [D, H1])
        last_col = sb("last_col", [D, 1])
        last_row = sb("last_row", [P, AW])
        bias_last = sb("bias_last", [D, 1])
        w1 = sb("w1", [P, 2 * H2])
        w2 = sb("w2", [P, 4])
        b0 = sb("b0", [P, 1])
        b1 = sb("b1", [P, 1])
        b2 = sb("b2", [P, 1])
        hl1 = sb("hl1", [D, N])
        hl2 = sb("hl2", [H2, N])
        mw0 = sb("mw0", [P, 2, M0])
        mw1 = sb("mw1", [P, 2, M1])
        mw2 = sb("mw2", [P, 1])
        mb0 = sb("mb0", [P, 2])
        mb1 = sb("mb1", [P, 1])
        mb2 = sb("mb2", [P, 1])

        psT = psum("psT", [P, 512])
        psL1 = psum("psL1", [P, 512])
        psL2 = psum("psL2", [P, 512])
        psS = psum("psS", [P, 512])
        psX = psum("psX", [P, 512])
        psM0 = psum("psM0", [P, 512])
        psM1 = psum("psM1", [P, 512])
        psY = psum("psY", [P, 512])

        ids_loaded = sem("ids_loaded")
        hist_loaded = sem("hist_loaded")
        consts_loaded = sem("consts_loaded")
        weights_loaded = sem("weights_loaded")
        dense_loaded = sem("dense_loaded")
        zeroed = sem("zeroed")
        ids_ready = sem("ids_ready")
        emb_gathered = sem("emb_gathered")
        side_gathered = sem("side_gathered")
        setup_dve = sem("setup_dve")
        setup_pe = sem("setup_pe")
        setup_act = sem("setup_act")
        plan_ready = sem("plan_ready")
        w_ready = sem("w_ready")
        sorted_ = sem("sorted_")
        sorting = sem("sorting")
        sort_step = sem("sort_step")
        prep_step = sem("prep_step")
        fin_step = sem("fin_step")
        soft_step = sem("soft_step")
        idx_loaded = [sem(f"idx_loaded{p}") for p in range(2)]
        gathered = [sem(f"gathered{p}") for p in range(2)]
        begun = sem("begun")
        landed = sem("landed")
        copied = sem("copied")
        transposed = sem("transposed")
        hT_ready = sem("hT_ready")
        pT_ready = sem("pT_ready")
        l1_done = sem("l1_done")
        h1_ready = sem("h1_ready")
        l2_done = sem("l2_done")
        h2_ready = sem("h2_ready")
        scored = sem("scored")
        scores_read = sem("scores_read")
        masked = sem("masked")
        weighted = sem("weighted")
        pooled = sem("pooled")
        x_ready = sem("x_ready")
        x_copied = sem("x_copied")
        xT_done = sem("xT_done")
        xT_ready = sem("xT_ready")
        m0_done = sem("m0_done")
        m0_ready = sem("m0_ready")
        m1_done = sem("m1_done")
        m1_ready = sem("m1_ready")
        y_done = sem("y_done")
        y_read = sem("y_read")
        probs_ready = sem("probs_ready")
        stored = sem("stored")

        def grouped(ap):
            return ap.rearrange("(p g) f -> p g f", g=G)

        def load_plan(eng, g):
            n = eng.value_load(plan[0:1, bass.ds(g, 1)], min_val=1, max_val=MAXC)
            before = eng.value_load(plan[0:1, bass.ds(g + 32, 1)], min_val=0, max_val=G * MAXC)
            return n, before

        block = ctx.enter_context(nc.Block())
        N_CONST, N_WEIGHT, N_DENSE = 2, 22, 2

        @block.sync
        def _(sp):
            for k, name in enumerate(("user_id", "item_id", "item_category", "item_dur_bkt")):
                sp.dma_start(raw_ids[:, k, :], a[name].rearrange("(p g) -> p g", g=G)).then_inc(ids_loaded, 16)
            sp.dma_start(hist_ids[:, 0:G, :], grouped(a["history"])).then_inc(hist_loaded, 16)
            sp.dma_start(ident[:, :], a["ident"]).then_inc(consts_loaded, 16)
            sp.dma_start(scan[:, :], a["scan"]).then_inc(consts_loaded, 16)
            sp.wait_ge(zeroed, 1)
            sp.dma_start(x_all[:, 1:G + 1, X_UD:X_UD + FU], grouped(a["user_dense"])).then_inc(dense_loaded, 16)
            sp.dma_start(x_all[:, 1:G + 1, X_ID:X_ID + FI], grouped(a["item_dense"])).then_inc(dense_loaded, 16)

            sp.wait_ge(plan_ready, 1)
            total = sp.value_load(plan[0:1, 32 + G:33 + G], min_val=G, max_val=G * MAXC)
            halves = sp.snap((total + 1) // 2)
            for p in range(2):
                sp.wait_ge(sorted_, p + 1)
                sp.dma_start(idx[p][:, :], rows_all[:, p * SLOTS:(p + 1) * SLOTS]).then_inc(idx_loaded[p], 16)
            with sp.Fori(0, halves) as i:
                for p in range(2):
                    sp.wait_ge(gathered[p], (i + 1) * (16 * SLOTS))
                    sp.sem_inc(landed, 1)
                    sp.wait_ge(sorted_, i * 2 + (3 + p))
                    sp.dma_start(idx[p][:, :], rows_all[:, bass.ds(i * (2 * SLOTS) + (2 + p) * SLOTS, SLOTS)]
                                 ).then_inc(idx_loaded[p], 16)
            last = sp.snap(halves * 16 + 16)
            for p in range(2):
                sp.wait_ge(idx_loaded[p], last)
            sp.wait_ge(probs_ready, 1)
            sp.dma_start(out.rearrange("(p g) -> p g", g=G), probs[:, :]).then_inc(stored, 16)
            sp.wait_ge(stored, 16)

        @block.gpsimd
        def _(pool):
            def rows(table, ids, dst):
                return pool.indirect_dma_start(
                    out=dst, out_offset=None, in_=table, in_offset=bass.IndirectOffsetOnAxis(ap=ids, axis=0))

            pool.wait_ge(ids_ready, 1)
            pool.wait_ge(zeroed, 1)
            for g in range(G):
                rows(a["item_W"], row_ids[:, 1, g:g + 1], x_all[:, g + 1, X_ITEM:X_ITEM + D]).then_inc(emb_gathered, 16)
            for g in range(G):
                rows(a["user_W"], row_ids[:, 0, g:g + 1], x_all[:, g + 1, X_USER:X_USER + D]).then_inc(side_gathered, 16)
                rows(a["cat_W"], row_ids[:, 2, g:g + 1], x_all[:, g + 1, X_CAT:X_CAT + DC]).then_inc(side_gathered, 16)
                rows(a["dur_W"], row_ids[:, 3, g:g + 1], x_all[:, g + 1, X_DUR:X_DUR + DD]).then_inc(side_gathered, 16)
            pool.wait_ge(plan_ready, 1)
            total = pool.value_load(plan[0:1, 32 + G:33 + G], min_val=G, max_val=G * MAXC)
            with pool.Fori(0, pool.snap((total + 1) // 2)) as i:
                for p in range(2):
                    pool.wait_ge(idx_loaded[p], (i + 1) * 16)
                    pool.wait_ge(copied, i * 4 + (2 * p + 2))
                    pool.sem_inc(begun, 1)
                    for j in range(SLOTS):
                        ins = pool.indirect_dma_start(
                            out=hist_in[:, p, j, :], out_offset=None, in_=a["hist_W"],
                            in_offset=bass.IndirectOffsetOnAxis(ap=idx[p][:, j:j + 1], axis=0))
                        ins.then_inc(gathered[p], 16)

        @block.scalar
        def _(act):
            wt = a["aW0"]
            Wh, Wt, Wp, Wd = (wt[k * D:(k + 1) * D, :] for k in range(4))
            act.wait_ge(zeroed, 1)
            n = 0

            def load(dst, src):
                act.dma_start(dst, src).then_inc(weights_loaded, 16)
                return 1

            for h in range(2):
                lo, hi = h * D, (h + 1) * D
                n += load(w_hist[lo:hi, lo:hi], Wh)
                n += load(w_diff[lo:hi, lo:hi], Wd)
                n += load(w_prod[lo:hi, lo:hi], Wp)
                n += load(w_item[0:D, lo:hi], Wt)
                n += load(w_item[D:P, lo:hi], Wd)
                n += load(w1[lo:hi, h * H2:(h + 1) * H2], a["aW1"])
                n += load(b0[lo:hi, :], a["ab0"].rearrange("(f o) -> f o", o=1))
            for q in range(4):
                n += load(w2[q * H2:(q + 1) * H2, q:q + 1], a["aW2"])
                n += load(b1[q * H2:(q + 1) * H2, :], a["ab1"].rearrange("(f o) -> f o", o=1))
            assert n == N_WEIGHT
            n += load(b2[:, :], a["ab2"].rearrange("(o f) -> o f", o=1).broadcast_to([P, 1]))
            n += load(w_diff_lo[:, :], Wd)
            n += load(last_col[:, :], a["hist_W"][LAST:LAST + 1, :].rearrange("o f -> f o"))
            n += load(last_row[:, 0:D], a["hist_W"][LAST:LAST + 1, :].broadcast_to([P, D]))
            n += load(mw0[:, 0, :], a["mW0"][0:P, :])
            n += load(mw0[0:XB, 1, :], a["mW0"][P:XW, :])
            for h in range(2):
                n += load(mw1[:, h, :], a["mW1"][h * P:(h + 1) * P, :])
                n += load(mb0[:, h:h + 1], a["mb0"][h * P:(h + 1) * P].rearrange("(f o) -> f o", o=1))
            n += load(mw2[:, :], a["mW2"])
            n += load(mb1[:, :], a["mb1"].rearrange("(f o) -> f o", o=1))
            n += load(mb2[:, :], a["mb2"].rearrange("(o f) -> o f", o=1).broadcast_to([P, 1]))
            assert n == N_WEIGHT + 13
            act.sem_inc(copied, 4)

            act.wait_ge(weights_loaded, 16 * n)
            act.wait_ge(setup_pe, 3)
            act.activation(bias_last[:, :], psM0[0:D, 0:1], ACT.Identity, bias=b0[0:D, :]).then_inc(setup_act, 1)
            for r in range(G // 4):
                act.wait_ge(setup_pe, 4 * r + 4)
                act.activation(itemT[0:D, r * N:(r + 1) * N], psT[0:D, :], ACT.Copy).then_inc(setup_act, 1)
                act.wait_ge(setup_pe, 4 * r + 5)
                act.wait_ge(setup_act, 3 * r + 1)
                act.activation(hl1[:, :], psL1[0:D, :], ACT.Relu, bias=bias_last[:, :]).then_inc(setup_act, 1)
                act.wait_ge(setup_pe, 4 * r + 6)
                act.activation(hl2[:, :], psL2[0:H2, :], ACT.Relu, bias=b1[0:H2, :]).then_inc(setup_act, 1)

            def mlp(slot, g1):
                act.wait_ge(dense_loaded, 16 * N_DENSE)
                act.wait_ge(x_ready, g1)
                act.activation(x_pe[:, :], x_all[:, slot, :] if isinstance(slot, int)
                               else x_all[:, bass.ds(slot, 1), :].rearrange("p o f -> p (o f)"),
                               ACT.Copy).then_inc(x_copied, 1)
                act.wait_ge(xT_done, g1)
                act.activation(xT[:, 0:P], psX[:, 0:P], ACT.Copy)
                act.activation(xT[0:XB, P:2 * P], psX[0:XB, P:2 * P], ACT.Copy).then_inc(xT_ready, 1)
                act.wait_ge(m0_done, g1)
                act.activation(m0[:, 0:P], psM0[:, 0:P], ACT.Relu, bias=mb0[:, 0:1])
                act.activation(m0[:, P:2 * P], psM0[:, P:2 * P], ACT.Relu, bias=mb0[:, 1:2]).then_inc(m0_ready, 1)
                act.wait_ge(m1_done, g1)
                act.activation(m1[:, :], psM1[:, 0:P], ACT.Relu, bias=mb1[:, :]).then_inc(m1_ready, 1)
                act.wait_ge(y_done, g1)
                dst = logits[:, slot:slot + 1] if isinstance(slot, int) else logits[:, bass.ds(slot, 1)]
                act.activation(dst, psY[:, 0:1], ACT.Copy).then_inc(y_read, 1)

            act.wait_ge(plan_ready, 1)
            act.wait_ge(side_gathered, 16 * 3 * G)
            with act.Fori(0, G) as g:
                chunks, before = load_plan(act, g)
                with act.Fori(0, chunks) as c:
                    t = act.snap(before + c)
                    half = act.snap(t % 2)
                    act.wait_ge(landed, t + 1)
                    act.wait_ge(transposed, t + 1)
                    src = hist_in[:, bass.ds(half, 1), :, :].rearrange("p o j d -> p (o j) d")
                    act.activation(hist_pe[:, :].rearrange("p (j d) -> p j d", d=D), src, ACT.Copy
                                   ).then_inc(copied, 1)
                    act.wait_ge(pooled, t + 1)
                    act.activation(rows_x[:, bass.ds(half, 1), 0:SLOTS, 0:D].rearrange("p o j d -> p (o j) d"),
                                   src, ACT.Copy).then_inc(copied, 1)
                    act.wait_ge(transposed, t + 2)
                    act.activation(hT[:, :], psT[:, :], ACT.Copy).then_inc(hT_ready, 1)
                    act.wait_ge(l1_done, t + 1)
                    act.activation(h1[:, :], psL1[:, :], ACT.Relu, bias=b0[:, :]).then_inc(h1_ready, 1)
                    act.wait_ge(l2_done, t + 1)
                    act.activation(h2[:, :], psL2[:, 0:N // 2], ACT.Relu, bias=b1[:, :]).then_inc(h2_ready, 1)
                    act.wait_ge(masked, t + 1)
                    act.activation(e9[:, :], score9[:, :], ACT.Exp, bias=neg_max[:, :]).then_inc(weighted, 1)
                mlp(g, g + 1)
            mlp(G, G + 1)
            act.wait_ge(y_read, G + 1)
            act.activation(probs[:, :], logits[:, 1:G + 1], ACT.Sigmoid, bias=mb2[:, :]).then_inc(probs_ready, 1)

        @block.tensor
        def _(pe):
            pe.wait_ge(consts_loaded, 16 * N_CONST)
            pe.wait_ge(setup_dve, 3)
            pe.transpose(psX[0:G, 0:P], row_count[:, :], ident[:, :]).then_inc(setup_pe, 1)
            pe.wait_ge(setup_dve, 7)
            pe.matmul(psX[0:1, P:P + 2 * G + 1], chunks_f[:, :], scan[:, :], start=True, stop=True
                      ).then_inc(setup_pe, 1)
            pe.wait_ge(w_ready, 1)
            pe.matmul(psM0[0:D, 0:1], w_hist[0:D, 0:D], last_col[:, :], start=True, stop=True
                      ).then_inc(setup_pe, 1)
            pe.wait_ge(emb_gathered, 16 * G)
            for r in range(G // 4):
                if r:
                    pe.wait_ge(setup_act, 3 * r - 1)
                    pe.wait_ge(w_ready, 1 + r)
                for q in range(4):
                    ins = pe.transpose(psT[0:D, q * P:(q + 1) * P], x_all[:, 4 * r + q + 1, X_ITEM:X_ITEM + D],
                                       ident[:, :])
                ins.then_inc(setup_pe, 1)
                pe.wait_ge(setup_act, 3 * r + 2)
                pe.matmul(psL1[0:D, :], w_last[:, :], itemT[0:D, r * N:(r + 1) * N], start=True, stop=True
                          ).then_inc(setup_pe, 1)
                pe.wait_ge(setup_act, 3 * r + 3)
                pe.matmul(psL2[0:H2, :], w1[0:D, 0:H2], hl1[:, :], start=True, stop=True).then_inc(setup_pe, 1)
                pe.wait_ge(setup_act, 3 * r + 4)
                for q in range(4):
                    ins = pe.matmul(psS[:, 16 + 4 * r + q:17 + 4 * r + q], hl2[:, q * P:(q + 1) * P], w2[0:H2, 0:1],
                                    start=True, stop=True)
                ins.then_inc(setup_pe, 1)
            pe.wait_ge(w_ready, 1 + G // 4)
            pe.sem_inc(transposed, 1)

            def mlp(g1):
                pe.wait_ge(x_copied, g1)
                pe.transpose(psX[:, 0:P], x_pe[:, 0:P], ident[:, :])
                pe.transpose(psX[0:XB, P:2 * P], x_pe[:, P:XW], ident[:, :]).then_inc(xT_done, 1)
                pe.wait_ge(xT_ready, g1)
                for h in range(2):
                    pe.matmul(psM0[:, h * P:(h + 1) * P], mw0[:, 0, h * P:(h + 1) * P], xT[:, 0:P],
                              start=True, stop=False)
                    ins = pe.matmul(psM0[:, h * P:(h + 1) * P], mw0[0:XB, 1, h * P:(h + 1) * P], xT[0:XB, P:2 * P],
                                    start=False, stop=True)
                ins.then_inc(m0_done, 1)
                pe.wait_ge(m0_ready, g1)
                for h in range(2):
                    ins = pe.matmul(psM1[:, 0:P], mw1[:, h, :], m0[:, h * P:(h + 1) * P],
                                    start=(h == 0), stop=(h == 1))
                ins.then_inc(m1_done, 1)
                pe.wait_ge(m1_ready, g1)
                pe.matmul(psY[:, 0:1], m1[:, :], mw2[:, :], start=True, stop=True).then_inc(y_done, 1)

            pe.wait_ge(plan_ready, 1)
            with pe.Fori(0, G) as g:
                chunks, before = load_plan(pe, g)
                item = itemT[:, bass.ds(g * P, P)].rearrange("p (o n) -> p o n", o=1).broadcast_to([P, PAIRS, P])
                with pe.Fori(0, chunks) as c:
                    t = pe.snap(before + c)
                    pe.wait_ge(copied, t * 2 + 5)
                    for q in range(PAIRS):
                        ins = pe.transpose(psT[:, q * P:(q + 1) * P], hist_pe[:, q * P:(q + 1) * P], ident[:, :])
                    ins.then_inc(transposed, 1)
                    pe.matmul(psL1[:, :].rearrange("p (q n) -> p q n", q=PAIRS), w_item[:, :], item,
                              start=True, stop=False)
                    pe.wait_ge(hT_ready, t + 1)
                    pe.matmul(psL1[:, :], w_hist[:, :], hT[:, :], start=False, stop=False)
                    pe.wait_ge(pT_ready, t + 1)
                    pe.matmul(psL1[:, :], w_prod[:, :], pT[:, :], start=False, stop=True).then_inc(l1_done, 1)
                    pe.wait_ge(h1_ready, t + 1)
                    for u in range(2):
                        ins = pe.matmul(psL2[u * 2 * H2:(u + 1) * 2 * H2, 0:2 * P], w1[:, :],
                                        h1[:, u * 2 * P:(u + 1) * 2 * P], start=True, stop=True)
                    ins.then_inc(l2_done, 1)
                    pe.wait_ge(h2_ready, t + 1)
                    pe.wait_ge(scores_read, t + 1)
                    for q in range(2):
                        dst = psS[:, 0:SLOTS].rearrange("p (u q e) -> p u q e", u=2, q=2)[:, :, q, :]
                        ins = pe.matmul(dst, h2[:, q * P:(q + 1) * P],
                                        w2[:, :].rearrange("p (u e) -> p u e", u=2), start=True, stop=True)
                    ins.then_inc(scored, 1)
                mlp(g + 1)
            mlp(G + 1)

        @block.vector
        def _(dve):
            step = [0]

            def chain(ins):
                step[0] += 1
                ins.then_inc(setup_dve, 1)
                dve.wait_ge(setup_dve, step[0])

            dve.memset(x_all[:, :, :], 0.0)
            dve.memset(rows_x[:, :, :, :], 1.0)
            for w in (w_hist, w_diff, w_prod, w1, w2):
                dve.memset(w[:, :], 0.0)
            dve.memset(last_row[:, D:AW], 1.0)
            dve.memset(vals_all[:, :], 0.0)
            dve.memset(hist_ids[:, G, :], LAST)
            dve.memset(logits[:, :], 0.0)
            dve.memset(plan[:, :], DUMMY)
            dve.memset(last_score[:, G:G + 1], 0.0).then_inc(zeroed, 1)
            dve.wait_ge(zeroed, 1)

            dve.wait_ge(ids_loaded, 64)
            sizes = (NU, NI, NC_, ND)
            for k in range(4):
                ins = dve.tensor_scalar(wrap_ids[:, k, :], raw_ids[:, k, :], 0.0, float(sizes[k]), ALU.is_lt, ALU.mult)
            chain(ins)
            ins = dve.tensor_tensor(wrap_ids[:, :, :], wrap_ids[:, :, :], raw_ids[:, :, :], ALU.add)
            chain(ins)
            for k in range(4):
                ins = dve.tensor_scalar(row_ids[:, k, :], wrap_ids[:, k, :], 0.0, float(sizes[k] - 1), ALU.max, ALU.min)
            ins.then_inc(ids_ready, 1)
            dve.wait_ge(hist_loaded, 16)
            dve.tensor_scalar(in_range[:, :, :], hist_ids[:, 0:G, :], float(LAST), None, ALU.is_lt
                              ).then_inc(prep_step, 1)
            dve.wait_ge(prep_step, 1)
            chain(dve.tensor_reduce(row_count[:, :], in_range[:, :, :], AX.X, ALU.add))
            dve.wait_ge(setup_pe, 1)
            chain(dve.tensor_reduce(max_col[:, :], psX[0:G, 0:P], AX.X, ALU.max))
            chain(dve.tensor_scalar(chunks_i[:, :], max_col[:, :], float(SLOTS - 1), None, ALU.add))
            chain(dve.tensor_scalar(chunks_i2[:, :], chunks_i[:, :], SLOTS.bit_length() - 1, None,
                                    ALU.logical_shift_right))
            chain(dve.tensor_scalar(chunks_f[:, :], chunks_i2[:, :], 1.0, None, ALU.max))
            assert step[0] == 7
            dve.wait_ge(setup_pe, 2)
            chain(dve.tensor_copy(plan[:, 0:G], psX[0:1, P:P + G]))
            dve.tensor_copy(plan[:, 32:33 + G], psX[0:1, P + G:P + 2 * G + 1]).then_inc(plan_ready, 1)
            dve.wait_ge(plan_ready, 1)

            PREP = 10

            def prepare(g, n0):
                ids = hist_ids[:, bass.ds(g, 1), :].rearrange("p o l -> p (o l)")
                dve.wait_ge(prep_step, n0)
                dve.tensor_scalar(key_wrap[:, :], ids, 0.0, float(LAST + 1), ALU.is_lt, ALU.mult
                                  ).then_inc(prep_step, 1)
                dve.wait_ge(prep_step, n0 + 1)
                dve.scalar_tensor_tensor(out=key_neg[:, :], in0=ids, scalar=-1.0, in1=key_wrap[:, :],
                                         op0=ALU.mult, op1=ALU.subtract).then_inc(prep_step, 1)
                dve.wait_ge(prep_step, n0 + 2)
                dve.tensor_scalar(key_wrap[:, :], key_neg[:, :], float(LAST), float(LAST), ALU.add, ALU.min
                                  ).then_inc(prep_step, 1)
                dve.wait_ge(prep_step, n0 + 3)
                dve.scalar_tensor_tensor(out=key[:, :], in0=ids, scalar=0.0, in1=key_wrap[:, :],
                                         op0=ALU.is_equal, op1=ALU.add).then_inc(prep_step, 1)
                dve.wait_ge(prep_step, n0 + 4)
                dve.tensor_scalar(key_neg[:, :], key[:, :], 0.0, None, ALU.is_gt).then_inc(prep_step, 1)
                dve.wait_ge(prep_step, n0 + 5)
                dve.tensor_reduce(n_real[:, :], key_neg[:, :], AX.X, ALU.add).then_inc(prep_step, 1)
                dve.wait_ge(prep_step, n0 + 6)
                dve.tensor_scalar(n_last[:, bass.ds(g, 1)], n_real[:, :], -1.0, float(L), ALU.mult, ALU.add)
                dve.tensor_scalar(has_last[:, :], n_real[:, :], float(L), None, ALU.is_lt).then_inc(prep_step, 1)
                dve.wait_ge(prep_step, n0 + 7)
                dve.tensor_scalar(has_pen[:, :], has_last[:, :], -ABSENT, ABSENT, ALU.mult, ALU.add
                                  ).then_inc(prep_step, 1)
                dve.tensor_tensor(last_kept[:, :], last_score[:, bass.ds(g, 1)], has_last[:, :], ALU.mult
                                  ).then_inc(prep_step, 1)
                dve.wait_ge(prep_step, n0 + 9)
                dve.tensor_tensor(last_start[:, bass.ds(g, 1)], last_kept[:, :], has_pen[:, :], ALU.add
                                  ).then_inc(prep_step, 1)

            def sort(before, chunks, prepared):
                with dve.Fori(0, chunks) as c:
                    k = dve.snap(before + c)
                    dve.wait_ge(prep_step, prepared)
                    dve.wait_ge(sort_step, k * 4 + 4)
                    dve.sem_inc(sorting, 1)
                    flat = bass.ds(k * SLOTS, SLOTS)
                    dve.max(top8[:, :], key[:, :]).then_inc(sort_step, 1)
                    dve.wait_ge(sort_step, k * 4 + 5)
                    dve.tensor_scalar(top8_row[:, :], top8[:, :], -1.0, float(LAST), ALU.mult, ALU.add
                                      ).then_inc(sort_step, 1)
                    dve.tensor_scalar(vals_all[:, flat], top8[:, :], 1.0, None, ALU.mult).then_inc(sort_step, 1)
                    dve.match_replace(key[:, :], top8[:, :], key[:, :], TAKEN).then_inc(sort_step, 1)
                    dve.wait_ge(sort_step, k * 4 + 8)
                    dve.tensor_scalar(rows_all[:, flat], top8_row[:, :], 0.0, float(LAST), ALU.max, ALU.min
                                      ).then_inc(sorted_, 1)

            def masks(before, n0, k_end):
                span = bass.ds(before * SLOTS, L)
                dve.wait_ge(sorted_, k_end)
                dve.tensor_scalar(pen_all[:, span], vals_all[:, span], 0.0, ABSENT, ALU.is_le, ALU.mult
                                  ).then_inc(prep_step, 1)
                dve.tensor_scalar(pen_pad[:, :], vals_all[:, span], float(LAST), MASKED, ALU.is_gt, ALU.mult
                                  ).then_inc(prep_step, 1)
                dve.wait_ge(prep_step, n0 + 2)
                dve.tensor_tensor(pen_all[:, span], pen_all[:, span], pen_pad[:, :], ALU.add
                                  ).then_inc(prep_step, 1)
                dve.wait_ge(prep_step, n0 + 3)
                dve.tensor_scalar(keep_all[:, span], pen_all[:, span], 0.0, None, ALU.is_equal
                                  ).then_inc(prep_step, 1)

            dve.wait_ge(weights_loaded, 16 * (N_WEIGHT + 13))
            dve.tensor_tensor(w_hist[:, :], w_hist[:, :], w_diff[:, :], ALU.add)
            dve.tensor_scalar(w_item[D:P, :], w_item[D:P, :], -1.0, None, ALU.mult)
            chain(dve.tensor_tensor(w_tmp[:, :], w_item[0:D, 0:D], w_diff_lo[:, :], ALU.subtract))
            dve.scalar_tensor_tensor(out=w_last[:, :], in0=w_prod[0:D, 0:D], scalar=last_col[:, :],
                                     in1=w_tmp[:, :], op0=ALU.mult, op1=ALU.add).then_inc(w_ready, 1)
            for r in range(G // 4):
                dve.wait_ge(setup_act, 3 * r + 2)
                dve.tensor_copy(itemT[D:P, r * N:(r + 1) * N], psT[0:D, :]).then_inc(w_ready, 1)
            dve.wait_ge(setup_pe, 4 * (G // 4) + 3)
            chain(dve.tensor_scalar(last_score[:, 0:G], psS[:, 16:16 + G], b2[:, :], None, ALU.add))

            def load_next(g):
                n = dve.value_load(plan[0:1, bass.ds(g, 1)], min_val=1, max_val=MAXC)
                b = dve.value_load(plan[0:1, bass.ds(g + 32, 1)], min_val=0, max_val=G * MAXC)
                return n, b

            dve.sem_inc(sort_step, 4)
            with dve.Fori(0, 1) as z:
                n0_, b0_ = load_next(z)
                prepare(z, z * (PREP + 4) + 1)
                sort(b0_, n0_, z + PREP + 1)
                masks(b0_, z * (PREP + 4) + 1 + PREP, n0_ + b0_)
            dve.sem_inc(scores_read, 1)
            dve.sem_inc(pooled, 2)

            def finish(slot, half, n0):
                acc = rows_x[:, bass.ds(half, 1), SLOTS, :].rearrange("p o f -> p (o f)")
                dve.wait_ge(fin_step, n0)
                dve.reciprocal(inv_sum[:, :], acc[:, D:AW]).then_inc(fin_step, 1)
                dve.wait_ge(fin_step, n0 + 1)
                dst = x_all[:, slot, X_POOL:XW] if isinstance(slot, int) else \
                    x_all[:, bass.ds(slot, 1), X_POOL:XW].rearrange("p o f -> p (o f)")
                dve.tensor_scalar(dst, acc[:, 0:D], inv_sum[:, :], None, ALU.mult).then_inc(x_ready, 1)
                return acc

            dve.sem_inc(fin_step, 1)
            with dve.Fori(0, G) as g:
                chunks, before = load_plan(dve, g)
                start = dve.snap(before % 2)
                dve.wait_ge(pooled, before + 2)
                acc = finish(g, start, g * 3 + 1)
                dve.wait_ge(x_ready, g + 1)
                dve.tensor_scalar(acc, last_row[:, :], n_last[:, bass.ds(g, 1)], None, ALU.mult).then_inc(fin_step, 1)
                dve.tensor_scalar(score9[:, SLOTS:SLOTS + 1], last_start[:, bass.ds(g, 1)], 1.0, None, ALU.mult
                                  ).then_inc(fin_step, 1)
                n1, b1_ = load_next(g + 1)
                prepare(g + 1, (g + 1) * (PREP + 4) + 1)
                sort(b1_, n1, (g + 1) * (PREP + 4) + (1 + PREP))
                masks(b1_, (g + 1) * (PREP + 4) + (1 + PREP), n1 + b1_)
                with dve.Fori(0, chunks) as c:
                    t = dve.snap(before + c)
                    half = dve.snap(t % 2)
                    other = dve.compute_val(dve.snap((t + 1) % 2))
                    flat = bass.ds(t * SLOTS, SLOTS)
                    dve.wait_ge(hT_ready, t + 1)
                    item = itemT[:, bass.ds(g * P, P)].rearrange("p (o n) -> p o n", o=1).broadcast_to([P, PAIRS, P])
                    dve.tensor_tensor(pT[:, :].rearrange("p (q n) -> p q n", q=PAIRS),
                                      psT[:, :].rearrange("p (q n) -> p q n", q=PAIRS), item, ALU.mult
                                      ).then_inc(pT_ready, 1)
                    dve.wait_ge(scored, t + 1)
                    dve.wait_ge(fin_step, g * 3 + 4)
                    dve.scalar_tensor_tensor(out=score9[:, 0:SLOTS], in0=psS[:, 0:SLOTS], scalar=b2[:, :],
                                             in1=keep_all[:, flat], op0=ALU.add, op1=ALU.mult
                                             ).then_inc(scores_read, 1)
                    dve.wait_ge(scores_read, t + 2)
                    dve.tensor_tensor(score9[:, 0:SLOTS], score9[:, 0:SLOTS], pen_all[:, flat], ALU.add
                                      ).then_inc(soft_step, 1)
                    dve.wait_ge(soft_step, t * 3 + 1)
                    dve.tensor_reduce(neg_max[:, :], score9[:, :], AX.X, ALU.max, negate=True).then_inc(masked, 1)
                    dve.wait_ge(weighted, t + 1)
                    dve.tensor_scalar(score9[:, SLOTS:SLOTS + 1], neg_max[:, :], -1.0, None, ALU.mult
                                      ).then_inc(soft_step, 1)
                    dve.wait_ge(copied, t * 2 + 6)
                    dve.tensor_tensor(prod[:, :, :],
                                      rows_x[:, bass.ds(half, 1), :, :].rearrange("p o j f -> p (o j) f"),
                                      e9[:, :].rearrange("p (j o) -> p j o", o=1).broadcast_to([P, SLOTS + 1, AW]),
                                      ALU.mult).then_inc(soft_step, 1)
                    dve.wait_ge(soft_step, t * 3 + 3)
                    dve.tensor_reduce(rows_x[:, bass.ds(other, 1), SLOTS, :].rearrange("p o f -> p (o f)"),
                                      prod[:, :, :].rearrange("p j f -> p f j"), AX.X, ALU.add).then_inc(pooled, 1)
                    dve.wait_ge(pooled, t + 3)
            with dve.Fori(0, 1) as z:
                total = dve.value_load(plan[0:1, bass.ds(z + (32 + G), 1)], min_val=G, max_val=G * MAXC)
                finish(G, dve.snap(total % 2), z + (G * 3 + 1))


_NAMES = {
    "user_dense": "r_user_dense", "user_id": "r_user_id", "item_id": "r_item_id",
    "item_category": "r_item_category", "item_dur_bkt": "r_item_dur_bkt", "item_dense": "r_item_dense",
    "history": "r_history_seq",
} | {n: f"L0_rec_{n}" for n in (
    "user_W", "item_W", "cat_W", "dur_W", "hist_W", "aW0", "ab0", "aW1", "ab1", "aW2", "ab2",
    "mW0", "mb0", "mW1", "mb1", "mW2", "mb2")}


def kernel(**inputs):
    import numpy as np
    import concourse.bacc as bacc
    from concourse.bass_utils import run_bass_kernel_spmd

    nc = bacc.Bacc("TRN2", target_bir_lowering=False, num_devices=1)
    arrays = {k: np.ascontiguousarray(inputs[name]) for k, name in _NAMES.items()}
    groups = arrays["history"].shape[0] // P
    arrays["ident"] = np.eye(P, dtype=np.float32)
    arrays["scan"] = np.concatenate(
        [np.eye(groups, dtype=np.float32), np.triu(np.ones((groups, groups + 1), np.float32), 1)], axis=1)
    args = {k: nc.dram_tensor(f"in_{k}", v.shape, mybir.dt.from_np(v.dtype), kind="ExternalInput").ap()
            for k, v in arrays.items()}
    out = nc.dram_tensor("out_y", [arrays["history"].shape[0]], F32, kind="ExternalOutput").ap()
    build(nc, args, out)
    r = run_bass_kernel_spmd(nc, [{f"in_{k}": v for k, v in arrays.items()}], core_ids=[0])
    return np.asarray(r.results[0]["out_y"])
```

```python
from contextlib import ExitStack

import concourse.bass as bass
from concourse import mybir

F32 = mybir.dt.float32
I32 = mybir.dt.int32
ALU = mybir.AluOpType
ACT = mybir.ActivationFunctionType
AX = mybir.AxisListType

P = 128
SLOTS = 8
PAIRS = SLOTS // 2
MASKED = -1.0e9
ABSENT = -3.0e9
MIN_CHUNKS = 2
PAD_KEY = 0.25


def build(nc, a, out):
    B, L = a["history"].shape
    LAST = a["hist_W"].shape[0] - 1
    D = a["hist_W"].shape[1]
    G = B // P
    MAXC = L // SLOTS
    LAST_KEY = -(LAST + 1.0)
    DUMMY = 4
    NK = (G * MAXC + MAXC) * SLOTS
    NU, NI = a["user_W"].shape[0], a["item_W"].shape[0]
    NC_, DC = a["cat_W"].shape
    ND, DD = a["dur_W"].shape
    H1, H2 = a["aW1"].shape
    FU, FI = a["user_dense"].shape[1], a["item_dense"].shape[1]
    M0, M1 = a["mW1"].shape
    X_USER, X_ITEM, X_CAT = 0, D, 2 * D
    X_DUR = X_CAT + DC
    X_UD = X_DUR + DD
    X_ID = X_UD + FU
    X_POOL = X_ID + FI
    XW = X_POOL + D
    XB = XW - P
    N = PAIRS * P
    AW = D + 1
    assert B % P == 0 and L % SLOTS == 0 and 2 * D == P and 4 * H2 == P and M0 == 2 * P and M1 == P

    ctx = ExitStack()
    with ctx:
        def sb(name, shape, dt=F32):
            return ctx.enter_context(nc.sbuf_tensor(name, shape, dt))

        def psum(name, shape):
            return ctx.enter_context(nc.psum_tensor(name, shape, F32))

        def sem(name):
            return ctx.enter_context(nc.semaphore(name))

        hist_nat = sb("hist_nat", [P, G, L], I32)
        hist_ids = sb("hist_ids", [P, G + 1, L], I32)
        raw_ids = sb("raw_ids", [P, 4, G], I32)
        row_nat = sb("row_nat", [P, 4, G])
        rank_rows = sb("rank_rows", [P, 4, G])
        row_ids = sb("row_ids", [P, 4, G], I32)
        lanes = sb("lanes", [P, G + 1])
        rank_key = sb("rank_key", [P, G])
        rank_left = sb("rank_left", [P, G])
        ranked = sb("ranked", [P, G])
        ranked_i = sb("ranked_i", [P, G], I32)
        count_i = sb("count_i", [P, G], I32)
        rank_count = sb("rank_count", [P, G])
        place_i = sb("place_i", [P, G], I32)
        hist_row = sb("hist_row", [P, G], I32)
        is_at = sb("is_at", [P, G, G])
        picked = sb("picked", [P, 4, G, G])
        dense_nat = sb("dense_nat", [P, G, FU + FI])
        dense_pick = sb("dense_pick", [P, 4, FU + FI, G])
        probs_pick = sb("probs_pick", [P, G, G])
        probs_nat = sb("probs_nat", [P, G])
        wrap_ids = sb("wrap_ids", [P, 4, G])
        in_range = sb("in_range", [P, G, L])
        row_count = sb("row_count", [P, G])
        max_col = sb("max_col", [G, 1])
        chunks_i = sb("chunks_i", [G, 1], I32)
        chunks_i2 = sb("chunks_i2", [G, 1], I32)
        chunks_f = sb("chunks_f", [G, 1])
        plan = sb("plan", [1, 64], I32)
        ident = sb("ident", [P, P])
        scan = sb("scan", [G, 2 * G + 1])
        key = sb("key", [P, L])
        key_wrap = sb("key_wrap", [P, L])
        key_row = sb("key_row", [P, L])
        top8 = sb("top8", [P, SLOTS])
        rows_all = sb("rows_all", [P, NK], I32)
        vals_all = sb("vals_all", [P, NK])
        keep_all = sb("keep_all", [P, NK])
        pen_all = sb("pen_all", [P, NK])
        pen_pad = sb("pen_pad", [P, L])
        n_last = sb("n_last", [P, G + 1])
        has_last = sb("has_last", [P, 1])
        has_pen = sb("has_pen", [P, 1])
        last_kept = sb("last_kept", [P, 1])
        last_start = sb("last_start", [P, G + 1])
        last_score = sb("last_score", [P, G + 1])
        idx = [sb(f"idx{p}", [P, SLOTS], I32) for p in range(2)]
        hist_in = sb("hist_in", [P, 2, SLOTS, D])
        hist_pe = sb("hist_pe", [P, SLOTS * D])
        rows_x = sb("rows_x", [P, 2, SLOTS + 1, AW])
        hT = sb("hT", [P, N])
        pT = sb("pT", [P, N])
        h1 = sb("h1", [P, N])
        h2 = sb("h2", [P, N // 2])
        score9 = sb("score9", [P, SLOTS + 1])
        neg_max = sb("neg_max", [P, 1])
        e9 = sb("e9", [P, SLOTS + 1])
        prod = sb("prod", [P, SLOTS + 1, AW])
        inv_sum = sb("inv_sum", [P, 1])
        itemT = sb("itemT", [P, G * P])
        x_all = sb("x_all", [P, G + 1, XW])
        x_pe = sb("x_pe", [P, XW])
        xT = sb("xT", [P, 2 * P])
        m0 = sb("m0", [P, 2 * P])
        m1 = sb("m1", [P, P])
        logits = sb("logits", [P, G + 1])
        probs = sb("probs", [P, G])
        w_hist = sb("w_hist", [P, P])
        w_diff = sb("w_diff", [P, P])
        w_prod = sb("w_prod", [P, P])
        w_item = sb("w_item", [P, P])
        w_last = sb("w_last", [D, H1])
        w_tmp = sb("w_tmp", [D, H1])
        w_diff_lo = sb("w_diff_lo", [D, H1])
        last_col = sb("last_col", [D, 1])
        last_row = sb("last_row", [P, AW])
        bias_last = sb("bias_last", [D, 1])
        w1 = sb("w1", [P, 2 * H2])
        w2 = sb("w2", [P, 4])
        b0 = sb("b0", [P, 1])
        b1 = sb("b1", [P, 1])
        b2 = sb("b2", [P, 1])
        hl1 = sb("hl1", [D, N])
        hl2 = sb("hl2", [H2, N])
        mw0 = sb("mw0", [P, 2, M0])
        mw1 = sb("mw1", [P, 2, M1])
        mw2 = sb("mw2", [P, 1])
        mb0 = sb("mb0", [P, 2])
        mb1 = sb("mb1", [P, 1])
        mb2 = sb("mb2", [P, 1])

        psT = psum("psT", [P, 512])
        psL1 = psum("psL1", [P, 512])
        psL2 = psum("psL2", [P, 512])
        psS = psum("psS", [P, 512])
        psX = psum("psX", [P, 512])
        psM0 = psum("psM0", [P, 512])
        psM1 = psum("psM1", [P, 512])
        psY = psum("psY", [P, 512])

        ids_loaded = sem("ids_loaded")
        hist_loaded = sem("hist_loaded")
        counts_ready = sem("counts_ready")
        chunks_ready = sem("chunks_ready")
        ranks_ready = sem("ranks_ready")
        hist0_gathered = sem("hist0_gathered")
        hist_gathered = sem("hist_gathered")
        consts_loaded = sem("consts_loaded")
        weights_loaded = sem("weights_loaded")
        dense_loaded = sem("dense_loaded")
        zeroed = sem("zeroed")
        ids_ready = sem("ids_ready")
        emb_gathered = sem("emb_gathered")
        side_gathered = sem("side_gathered")
        setup_dve = sem("setup_dve")
        setup_pe = sem("setup_pe")
        setup_act = sem("setup_act")
        plan_ready = sem("plan_ready")
        w_ready = sem("w_ready")
        sorted_ = sem("sorted_")
        sorting = sem("sorting")
        sort_chain = sem("sort_chain")
        prep_step = sem("prep_step")
        fin_step = sem("fin_step")
        soft_step = sem("soft_step")
        idx_loaded = [sem(f"idx_loaded{p}") for p in range(2)]
        gathered = [sem(f"gathered{p}") for p in range(2)]
        begun = sem("begun")
        landed = sem("landed")
        copied = sem("copied")
        transposed = sem("transposed")
        hT_ready = sem("hT_ready")
        pT_ready = sem("pT_ready")
        l1_done = sem("l1_done")
        h1_ready = sem("h1_ready")
        l2_done = sem("l2_done")
        h2_ready = sem("h2_ready")
        scored = sem("scored")
        scores_read = sem("scores_read")
        masked = sem("masked")
        weighted = sem("weighted")
        pooled = sem("pooled")
        x_ready = sem("x_ready")
        x_copied = sem("x_copied")
        xT_done = sem("xT_done")
        xT_ready = sem("xT_ready")
        m0_done = sem("m0_done")
        m0_ready = sem("m0_ready")
        m1_done = sem("m1_done")
        m1_ready = sem("m1_ready")
        y_done = sem("y_done")
        y_read = sem("y_read")
        probs_ready = sem("probs_ready")
        stored = sem("stored")

        def grouped(ap):
            return ap.rearrange("(p g) f -> p g f", g=G)

        def load_plan(eng, g):
            n = eng.value_load(plan[0:1, bass.ds(g, 1)], min_val=MIN_CHUNKS, max_val=MAXC)
            before = eng.value_load(plan[0:1, bass.ds(g + 32, 1)], min_val=0, max_val=G * MAXC)
            return n, before

        block = ctx.enter_context(nc.Block())
        N_CONST, N_WEIGHT, N_DENSE = 3, 22, 2

        @block.sync
        def _(sp):
            for k, name in enumerate(("user_id", "item_id", "item_category", "item_dur_bkt")):
                sp.dma_start(raw_ids[:, k, :], a[name].rearrange("(p g) -> p g", g=G)).then_inc(ids_loaded, 16)
            sp.dma_start(hist_nat[:, :, :], grouped(a["history"])).then_inc(hist_loaded, 16)
            sp.dma_start(ident[:, :], a["ident"]).then_inc(consts_loaded, 16)
            sp.dma_start(scan[:, :], a["scan"]).then_inc(consts_loaded, 16)
            sp.dma_start(lanes[:, :], a["lanes"]).then_inc(consts_loaded, 16)
            sp.dma_start(dense_nat[:, :, 0:FU], grouped(a["user_dense"])).then_inc(dense_loaded, 16)
            sp.dma_start(dense_nat[:, :, FU:FU + FI], grouped(a["item_dense"])).then_inc(dense_loaded, 16)

            sp.wait_ge(plan_ready, 1)
            total = sp.value_load(plan[0:1, 32 + G:33 + G], min_val=G * MIN_CHUNKS, max_val=G * MAXC)
            halves = sp.snap((total + 1) // 2)
            for p in range(2):
                sp.wait_ge(sorted_, p + 1)
                sp.dma_start(idx[p][:, :], rows_all[:, p * SLOTS:(p + 1) * SLOTS]).then_inc(idx_loaded[p], 16)
            with sp.Fori(0, halves) as i:
                for p in range(2):
                    sp.wait_ge(gathered[p], (i + 1) * (16 * SLOTS))
                    sp.sem_inc(landed, 1)
                    sp.wait_ge(sorted_, i * 2 + (3 + p))
                    sp.dma_start(idx[p][:, :], rows_all[:, bass.ds(i * (2 * SLOTS) + (2 + p) * SLOTS, SLOTS)]
                                 ).then_inc(idx_loaded[p], 16)
            sp.sem_inc(landed, 1)
            last = sp.snap(halves * 16 + 16)
            for p in range(2):
                sp.wait_ge(idx_loaded[p], last)
            sp.wait_ge(probs_ready, 2)
            sp.dma_start(out.rearrange("(p g) -> p g", g=G), probs_nat[:, :]).then_inc(stored, 16)
            sp.wait_ge(stored, 16)

        @block.gpsimd
        def _(pool):
            def rows(table, ids, dst):
                return pool.indirect_dma_start(
                    out=dst, out_offset=None, in_=table, in_offset=bass.IndirectOffsetOnAxis(ap=ids, axis=0))

            pool.wait_ge(ranks_ready, 1)
            for g in range(G):
                rows(a["history"], hist_row[:, g:g + 1], hist_ids[:, g, :]
                     ).then_inc(hist_gathered if g else hist0_gathered, 16)
            pool.wait_ge(ids_ready, 1)
            for g in range(G):
                rows(a["item_W"], row_ids[:, 1, g:g + 1], x_all[:, g + 1, X_ITEM:X_ITEM + D]).then_inc(emb_gathered, 16)
            for g in range(G):
                rows(a["user_W"], row_ids[:, 0, g:g + 1], x_all[:, g + 1, X_USER:X_USER + D]).then_inc(side_gathered, 16)
                rows(a["cat_W"], row_ids[:, 2, g:g + 1], x_all[:, g + 1, X_CAT:X_CAT + DC]).then_inc(side_gathered, 16)
                rows(a["dur_W"], row_ids[:, 3, g:g + 1], x_all[:, g + 1, X_DUR:X_DUR + DD]).then_inc(side_gathered, 16)
            pool.wait_ge(plan_ready, 1)
            total = pool.value_load(plan[0:1, 32 + G:33 + G], min_val=G * MIN_CHUNKS, max_val=G * MAXC)
            with pool.Fori(0, pool.snap((total + 1) // 2)) as i:
                for p in range(2):
                    pool.wait_ge(idx_loaded[p], (i + 1) * 16)
                    pool.wait_ge(copied, i * 4 + (2 * p + 2))
                    pool.sem_inc(begun, 1)
                    for j in range(SLOTS):
                        ins = pool.indirect_dma_start(
                            out=hist_in[:, p, j, :], out_offset=None, in_=a["hist_W"],
                            in_offset=bass.IndirectOffsetOnAxis(ap=idx[p][:, j:j + 1], axis=0))
                        ins.then_inc(gathered[p], 16)

        @block.scalar
        def _(act):
            wt = a["aW0"]
            Wh, Wt, Wp, Wd = (wt[k * D:(k + 1) * D, :] for k in range(4))
            act.wait_ge(zeroed, 1)
            n = 0

            def load(dst, src):
                act.dma_start(dst, src).then_inc(weights_loaded, 16)
                return 1

            for h in range(2):
                lo, hi = h * D, (h + 1) * D
                n += load(w_hist[lo:hi, lo:hi], Wh)
                n += load(w_diff[lo:hi, lo:hi], Wd)
                n += load(w_prod[lo:hi, lo:hi], Wp)
                n += load(w_item[0:D, lo:hi], Wt)
                n += load(w_item[D:P, lo:hi], Wd)
                n += load(w1[lo:hi, h * H2:(h + 1) * H2], a["aW1"])
                n += load(b0[lo:hi, :], a["ab0"].rearrange("(f o) -> f o", o=1))
            for q in range(4):
                n += load(w2[q * H2:(q + 1) * H2, q:q + 1], a["aW2"])
                n += load(b1[q * H2:(q + 1) * H2, :], a["ab1"].rearrange("(f o) -> f o", o=1))
            assert n == N_WEIGHT
            n += load(b2[:, :], a["ab2"].rearrange("(o f) -> o f", o=1).broadcast_to([P, 1]))
            n += load(w_diff_lo[:, :], Wd)
            n += load(last_col[:, :], a["hist_W"][LAST:LAST + 1, :].rearrange("o f -> f o"))
            n += load(last_row[:, 0:D], a["hist_W"][LAST:LAST + 1, :].broadcast_to([P, D]))
            n += load(mw0[:, 0, :], a["mW0"][0:P, :])
            n += load(mw0[0:XB, 1, :], a["mW0"][P:XW, :])
            for h in range(2):
                n += load(mw1[:, h, :], a["mW1"][h * P:(h + 1) * P, :])
                n += load(mb0[:, h:h + 1], a["mb0"][h * P:(h + 1) * P].rearrange("(f o) -> f o", o=1))
            n += load(mw2[:, :], a["mW2"])
            n += load(mb1[:, :], a["mb1"].rearrange("(f o) -> f o", o=1))
            n += load(mb2[:, :], a["mb2"].rearrange("(o f) -> o f", o=1).broadcast_to([P, 1]))
            assert n == N_WEIGHT + 13
            act.sem_inc(copied, 4)

            act.wait_ge(weights_loaded, 16 * n)
            act.wait_ge(setup_pe, 3)
            act.activation(bias_last[:, :], psM0[0:D, 0:1], ACT.Identity, bias=b0[0:D, :]).then_inc(setup_act, 1)
            for r in range(G // 4):
                act.wait_ge(setup_pe, 4 * r + 4)
                act.activation(itemT[0:D, r * N:(r + 1) * N], psT[0:D, :], ACT.Copy).then_inc(setup_act, 1)
                act.wait_ge(setup_pe, 4 * r + 5)
                act.wait_ge(setup_act, 3 * r + 1)
                act.activation(hl1[:, :], psL1[0:D, :], ACT.Relu, bias=bias_last[:, :]).then_inc(setup_act, 1)
                act.wait_ge(setup_pe, 4 * r + 6)
                act.activation(hl2[:, :], psL2[0:H2, :], ACT.Relu, bias=b1[0:H2, :]).then_inc(setup_act, 1)

            def mlp(slot, g1):
                act.wait_ge(x_ready, g1)
                act.activation(x_pe[:, :], x_all[:, slot, :] if isinstance(slot, int)
                               else x_all[:, bass.ds(slot, 1), :].rearrange("p o f -> p (o f)"),
                               ACT.Copy).then_inc(x_copied, 1)
                act.wait_ge(xT_done, g1)
                act.activation(xT[:, 0:P], psX[:, 0:P], ACT.Copy)
                act.activation(xT[0:XB, P:2 * P], psX[0:XB, P:2 * P], ACT.Copy).then_inc(xT_ready, 1)
                act.wait_ge(m0_done, g1)
                act.activation(m0[:, 0:P], psM0[:, 0:P], ACT.Relu, bias=mb0[:, 0:1])
                act.activation(m0[:, P:2 * P], psM0[:, P:2 * P], ACT.Relu, bias=mb0[:, 1:2]).then_inc(m0_ready, 1)
                act.wait_ge(m1_done, g1)
                act.activation(m1[:, :], psM1[:, 0:P], ACT.Relu, bias=mb1[:, :]).then_inc(m1_ready, 1)
                act.wait_ge(y_done, g1)
                dst = logits[:, slot:slot + 1] if isinstance(slot, int) else logits[:, bass.ds(slot, 1)]
                act.activation(dst, psY[:, 0:1], ACT.Copy).then_inc(y_read, 1)

            act.sem_inc(weighted, 1)
            act.wait_ge(side_gathered, 16 * 3 * G)

            def rows_of(half):
                if isinstance(half, int):
                    return hist_in[:, half, :, :], rows_x[:, half, 0:SLOTS, 0:D]
                return (hist_in[:, bass.ds(half, 1), :, :].rearrange("p o j d -> p (o j) d"),
                        rows_x[:, bass.ds(half, 1), 0:SLOTS, 0:D].rearrange("p o j d -> p (o j) d"))

            def copy_hist(half):
                act.activation(hist_pe[:, :].rearrange("p (j d) -> p j d", d=D), rows_of(half)[0], ACT.Copy
                               ).then_inc(copied, 1)

            def copy_rows(half):
                src, dst = rows_of(half)
                act.activation(dst, src, ACT.Copy).then_inc(copied, 1)

            act.wait_ge(landed, 1)
            copy_hist(0)
            copy_rows(0)
            act.wait_ge(transposed, 1)
            act.activation(hT[:, :], psT[:, :], ACT.Copy).then_inc(hT_ready, 1)
            with act.Fori(0, G) as g:
                chunks, before = load_plan(act, g)
                with act.Fori(0, chunks) as c:
                    t = act.snap(before + c)
                    other = act.snap((t + 1) % 2)
                    act.wait_ge(landed, t + 2)
                    act.wait_ge(transposed, t + 1)
                    copy_hist(other)
                    act.wait_ge(l1_done, t + 1)
                    act.activation(h1[:, :], psL1[:, :], ACT.Relu, bias=b0[:, :]).then_inc(h1_ready, 1)
                    act.wait_ge(transposed, t + 2)
                    act.activation(hT[:, :], psT[:, :], ACT.Copy).then_inc(hT_ready, 1)
                    act.wait_ge(l2_done, t + 1)
                    act.activation(h2[:, :], psL2[:, 0:N // 2], ACT.Relu, bias=b1[:, :]).then_inc(h2_ready, 1)
                    act.wait_ge(pooled, t + 2)
                    copy_rows(other)
                    act.wait_ge(masked, t + 1)
                    act.activation(e9[:, :], score9[:, :], ACT.Exp, bias=neg_max[:, :]).then_inc(weighted, 1)
                mlp(g, g + 1)
            mlp(G, G + 1)
            act.wait_ge(y_read, G + 1)
            act.activation(probs[:, :], logits[:, 1:G + 1], ACT.Sigmoid, bias=mb2[:, :]).then_inc(probs_ready, 1)

        @block.tensor
        def _(pe):
            pe.wait_ge(consts_loaded, 16 * N_CONST)
            pe.wait_ge(counts_ready, 1)
            pe.transpose(psX[0:G, 0:P], rank_count[:, :], ident[:, :]).then_inc(setup_pe, 1)
            pe.wait_ge(chunks_ready, 1)
            pe.matmul(psX[0:1, P:P + 2 * G + 1], chunks_f[:, :], scan[:, :], start=True, stop=True
                      ).then_inc(setup_pe, 1)
            pe.wait_ge(w_ready, 1)
            pe.matmul(psM0[0:D, 0:1], w_hist[0:D, 0:D], last_col[:, :], start=True, stop=True
                      ).then_inc(setup_pe, 1)
            pe.wait_ge(emb_gathered, 16 * G)
            for r in range(G // 4):
                if r:
                    pe.wait_ge(setup_act, 3 * r - 1)
                    pe.wait_ge(w_ready, 1 + r)
                for q in range(4):
                    ins = pe.transpose(psT[0:D, q * P:(q + 1) * P], x_all[:, 4 * r + q + 1, X_ITEM:X_ITEM + D],
                                       ident[:, :])
                ins.then_inc(setup_pe, 1)
                pe.wait_ge(setup_act, 3 * r + 2)
                pe.matmul(psL1[0:D, :], w_last[:, :], itemT[0:D, r * N:(r + 1) * N], start=True, stop=True
                          ).then_inc(setup_pe, 1)
                pe.wait_ge(setup_act, 3 * r + 3)
                pe.matmul(psL2[0:H2, :], w1[0:D, 0:H2], hl1[:, :], start=True, stop=True).then_inc(setup_pe, 1)
                pe.wait_ge(setup_act, 3 * r + 4)
                for q in range(4):
                    ins = pe.matmul(psS[:, 16 + 4 * r + q:17 + 4 * r + q], hl2[:, q * P:(q + 1) * P], w2[0:H2, 0:1],
                                    start=True, stop=True)
                ins.then_inc(setup_pe, 1)
            pe.wait_ge(w_ready, 1 + G // 4)

            def transpose_rows():
                for q in range(PAIRS):
                    ins = pe.transpose(psT[:, q * P:(q + 1) * P], hist_pe[:, q * P:(q + 1) * P], ident[:, :])
                ins.then_inc(transposed, 1)

            def mlp(g1):
                pe.wait_ge(x_copied, g1)
                pe.transpose(psX[:, 0:P], x_pe[:, 0:P], ident[:, :])
                pe.transpose(psX[0:XB, P:2 * P], x_pe[:, P:XW], ident[:, :]).then_inc(xT_done, 1)
                pe.wait_ge(xT_ready, g1)
                for h in range(2):
                    pe.matmul(psM0[:, h * P:(h + 1) * P], mw0[:, 0, h * P:(h + 1) * P], xT[:, 0:P],
                              start=True, stop=False)
                    ins = pe.matmul(psM0[:, h * P:(h + 1) * P], mw0[0:XB, 1, h * P:(h + 1) * P], xT[0:XB, P:2 * P],
                                    start=False, stop=True)
                ins.then_inc(m0_done, 1)
                pe.wait_ge(m0_ready, g1)
                for h in range(2):
                    ins = pe.matmul(psM1[:, 0:P], mw1[:, h, :], m0[:, h * P:(h + 1) * P],
                                    start=(h == 0), stop=(h == 1))
                ins.then_inc(m1_done, 1)
                pe.wait_ge(m1_ready, g1)
                pe.matmul(psY[:, 0:1], m1[:, :], mw2[:, :], start=True, stop=True).then_inc(y_done, 1)

            pe.wait_ge(plan_ready, 1)
            pe.wait_ge(copied, 5)
            transpose_rows()
            with pe.Fori(0, G) as g:
                chunks, before = load_plan(pe, g)
                item = itemT[:, bass.ds(g * P, P)].rearrange("p (o n) -> p o n", o=1).broadcast_to([P, PAIRS, P])
                with pe.Fori(0, chunks) as c:
                    t = pe.snap(before + c)
                    pe.matmul(psL1[:, :].rearrange("p (q n) -> p q n", q=PAIRS), w_item[:, :], item,
                              start=True, stop=False)
                    pe.wait_ge(hT_ready, t + 1)
                    pe.matmul(psL1[:, :], w_hist[:, :], hT[:, :], start=False, stop=False)
                    pe.wait_ge(pT_ready, t + 1)
                    pe.matmul(psL1[:, :], w_prod[:, :], pT[:, :], start=False, stop=True).then_inc(l1_done, 1)
                    pe.wait_ge(copied, t * 2 + 7)
                    transpose_rows()
                    pe.wait_ge(h1_ready, t + 1)
                    for u in range(2):
                        ins = pe.matmul(psL2[u * 2 * H2:(u + 1) * 2 * H2, 0:2 * P], w1[:, :],
                                        h1[:, u * 2 * P:(u + 1) * 2 * P], start=True, stop=True)
                    ins.then_inc(l2_done, 1)
                    pe.wait_ge(h2_ready, t + 1)
                    pe.wait_ge(scores_read, t + 1)
                    for q in range(2):
                        dst = psS[:, 0:SLOTS].rearrange("p (u q e) -> p u q e", u=2, q=2)[:, :, q, :]
                        ins = pe.matmul(dst, h2[:, q * P:(q + 1) * P],
                                        w2[:, :].rearrange("p (u e) -> p u e", u=2), start=True, stop=True)
                    ins.then_inc(scored, 1)
                mlp(g + 1)
            mlp(G + 1)

        @block.vector
        def _(dve):
            step = [0]

            def chain(ins):
                step[0] += 1
                ins.then_inc(setup_dve, 1)
                dve.wait_ge(setup_dve, step[0])

            dve.memset(x_all[:, 0, :], 0.0)
            dve.memset(e9[:, :], 1.0)
            dve.memset(neg_max[:, :], 0.0)
            dve.memset(rows_x[:, :, :, :], 1.0)
            for w in (w_hist, w_diff, w_prod, w1, w2):
                dve.memset(w[:, :], 0.0)
            dve.memset(last_row[:, D:AW], 1.0)
            dve.memset(vals_all[:, :], LAST_KEY)
            dve.memset(hist_ids[:, G, :], LAST)
            dve.memset(logits[:, :], 0.0)
            dve.memset(plan[:, :], DUMMY)
            dve.memset(last_score[:, G:G + 1], 0.0).then_inc(zeroed, 1)
            dve.wait_ge(zeroed, 1)

            dve.wait_ge(ids_loaded, 64)
            sizes = (NU, NI, NC_, ND)
            for k in range(4):
                ins = dve.tensor_scalar(wrap_ids[:, k, :], raw_ids[:, k, :], 0.0, float(sizes[k]), ALU.is_lt, ALU.mult)
            chain(ins)
            chain(dve.tensor_tensor(wrap_ids[:, :, :], wrap_ids[:, :, :], raw_ids[:, :, :], ALU.add))
            for k in range(4):
                ins = dve.tensor_scalar(row_nat[:, k, :], wrap_ids[:, k, :], 0.0, float(sizes[k] - 1), ALU.max, ALU.min)
            chain(ins)
            dve.wait_ge(hist_loaded, 16)
            chain(dve.tensor_scalar(in_range[:, :, :], hist_nat[:, :, :], float(LAST), None, ALU.is_lt))
            chain(dve.tensor_reduce(row_count[:, :], in_range[:, :, :], AX.X, ALU.add))
            dve.wait_ge(consts_loaded, 16 * N_CONST)
            chain(dve.scalar_tensor_tensor(out=rank_key[:, :], in0=row_count[:, :], scalar=float(G),
                                           in1=lanes[:, 0:G], op0=ALU.mult, op1=ALU.add))
            chain(dve.max(ranked[:, 0:8], rank_key[:, :]))
            chain(dve.match_replace(rank_left[:, :], ranked[:, 0:8], rank_key[:, :], -1.0))
            chain(dve.max(ranked[:, 8:16], rank_left[:, :]))
            chain(dve.tensor_copy(ranked_i[:, :], ranked[:, :]))
            dve.tensor_scalar(count_i[:, :], ranked_i[:, :], G.bit_length() - 1, None, ALU.logical_shift_right)
            chain(dve.tensor_scalar(place_i[:, :], ranked_i[:, :], G - 1, None, ALU.bitwise_and))
            dve.tensor_copy(rank_count[:, :], count_i[:, :]).then_inc(counts_ready, 1)
            dve.tensor_scalar(hist_row[:, :], place_i[:, :], lanes[:, G:G + 1], None, ALU.add
                              ).then_inc(ranks_ready, 1)
            chain(dve.tensor_tensor(
                is_at[:, :, :], ranked[:, :].rearrange("p (r o) -> p r o", o=1).broadcast_to([P, G, G]),
                rank_key[:, :].rearrange("p (o g) -> p o g", o=1).broadcast_to([P, G, G]), ALU.is_equal))
            for k in range(4):
                ins = dve.tensor_tensor(
                    picked[:, k, :, :], is_at[:, :, :],
                    row_nat[:, k, :].rearrange("p (o g) -> p o g", o=1).broadcast_to([P, G, G]), ALU.mult)
            chain(ins)
            chain(dve.tensor_reduce(rank_rows[:, :, :], picked[:, :, :, :], AX.X, ALU.add))
            dve.tensor_copy(row_ids[:, :, :], rank_rows[:, :, :]).then_inc(ids_ready, 1)
            dve.wait_ge(setup_pe, 1)
            chain(dve.tensor_reduce(max_col[:, :], psX[0:G, 0:P], AX.X, ALU.max))
            chain(dve.tensor_scalar(chunks_i[:, :], max_col[:, :], float(SLOTS - 1), None, ALU.add))
            chain(dve.tensor_scalar(chunks_i2[:, :], chunks_i[:, :], SLOTS.bit_length() - 1, None,
                                    ALU.logical_shift_right))
            dve.tensor_scalar(chunks_f[:, :], chunks_i2[:, :], float(MIN_CHUNKS), None, ALU.max
                              ).then_inc(chunks_ready, 1)
            dve.wait_ge(setup_pe, 2)
            chain(dve.tensor_copy(plan[:, 0:G], psX[0:1, P:P + G]))
            dve.tensor_copy(plan[:, 32:33 + G], psX[0:1, P + G:P + 2 * G + 1]).then_inc(plan_ready, 1)
            dve.wait_ge(plan_ready, 1)

            PREP = 8

            def prepare(g, n0):
                ids = hist_ids[:, bass.ds(g, 1), :].rearrange("p o l -> p (o l)")
                dve.wait_ge(prep_step, n0)
                dve.tensor_scalar(key_wrap[:, :], ids, 0.0, float(LAST + 1), ALU.is_lt, ALU.mult
                                  ).then_inc(prep_step, 1)
                dve.wait_ge(prep_step, n0 + 1)
                dve.tensor_tensor(key_row[:, :], ids, key_wrap[:, :], ALU.add).then_inc(prep_step, 1)
                dve.wait_ge(prep_step, n0 + 2)
                dve.tensor_scalar(key_wrap[:, :], key_row[:, :], 0.0, float(LAST), ALU.max, ALU.min
                                  ).then_inc(prep_step, 1)
                dve.wait_ge(prep_step, n0 + 3)
                dve.tensor_scalar(key_row[:, :], key_wrap[:, :], -1.0, -1.0, ALU.mult, ALU.add
                                  ).then_inc(prep_step, 1)
                dve.tensor_scalar(pen_pad[:, :], ids, 0.0, PAD_KEY, ALU.is_equal, ALU.mult
                                  ).then_inc(prep_step, 1)
                dve.wait_ge(prep_step, n0 + 5)
                dve.tensor_tensor(key[:, :], key_row[:, :], pen_pad[:, :], ALU.add).then_inc(prep_step, 1)
                dve.wait_ge(prep_step, n0 + 6)
                dve.tensor_scalar(key_row[:, :], key[:, :], LAST_KEY, None, ALU.is_le).then_inc(prep_step, 1)
                dve.wait_ge(prep_step, n0 + 7)
                dve.tensor_reduce(n_last[:, bass.ds(g, 1)], key_row[:, :], AX.X, ALU.add).then_inc(prep_step, 1)

            def sort_step(k):
                flat = bass.ds(k * SLOTS, SLOTS)
                dve.max(top8[:, :], key[:, :]).then_inc(sort_chain, 1)
                dve.wait_ge(sort_chain, k * 3 + 1)
                dve.tensor_scalar(rows_all[:, flat], top8[:, :], -1.0, -1.0, ALU.mult, ALU.add
                                  ).then_inc(sorted_, 1)
                dve.tensor_scalar(vals_all[:, flat], top8[:, :], 1.0, None, ALU.mult).then_inc(sort_chain, 1)
                dve.match_replace(key[:, :], top8[:, :], key[:, :], LAST_KEY).then_inc(sort_chain, 1)
                dve.wait_ge(sort_chain, k * 3 + 3)
                dve.sem_inc(sorting, 1)

            def masks(before, n0, k_end):
                span = bass.ds(before * SLOTS, L)
                dve.wait_ge(sort_chain, k_end * 3)
                dve.tensor_scalar(pen_all[:, span], vals_all[:, span], LAST_KEY, ABSENT, ALU.is_le, ALU.mult
                                  ).then_inc(prep_step, 1)
                dve.tensor_scalar(pen_pad[:, :], vals_all[:, span], PAD_KEY / 2 - 1, MASKED, ALU.is_gt, ALU.mult
                                  ).then_inc(prep_step, 1)
                dve.wait_ge(prep_step, n0 + 2)
                dve.tensor_tensor(pen_all[:, span], pen_all[:, span], pen_pad[:, :], ALU.add
                                  ).then_inc(prep_step, 1)
                dve.wait_ge(prep_step, n0 + 3)
                dve.tensor_scalar(keep_all[:, span], pen_all[:, span], 0.0, None, ALU.is_equal
                                  ).then_inc(prep_step, 1)

            START = 4

            def start_score(g, n0):
                n = n_last[:, bass.ds(g, 1)]
                dve.tensor_scalar(has_last[:, :], n, 0.0, None, ALU.is_gt).then_inc(prep_step, 1)
                dve.wait_ge(prep_step, n0 + 1)
                dve.tensor_scalar(has_pen[:, :], has_last[:, :], -ABSENT, ABSENT, ALU.mult, ALU.add
                                  ).then_inc(prep_step, 1)
                dve.tensor_tensor(last_kept[:, :], last_score[:, bass.ds(g, 1)], has_last[:, :], ALU.mult
                                  ).then_inc(prep_step, 1)
                dve.wait_ge(prep_step, n0 + 3)
                dve.tensor_tensor(last_start[:, bass.ds(g, 1)], last_kept[:, :], has_pen[:, :], ALU.add
                                  ).then_inc(prep_step, 1)

            PER_GROUP = PREP + 4 + START
            dve.sem_inc(prep_step, 1)
            FIRST = 1
            dve.wait_ge(hist0_gathered, 16)
            with dve.Fori(0, 1) as z:
                n_first, k_first = load_plan(dve, z)
                prepare(z, z + FIRST)
                dve.wait_ge(prep_step, z + (FIRST + PREP))
                dve.sem_inc(sorting, 1)
                with dve.Fori(0, n_first) as c:
                    sort_step(k_first + c)
                masks(k_first, z + (FIRST + PREP), k_first + n_first)

            dve.wait_ge(dense_loaded, 16 * N_DENSE)
            for r in range(0, G, 4):
                chain(dve.tensor_tensor(
                    dense_pick[:, :, :, :],
                    dense_nat[:, :, :].rearrange("p g (o f) -> p o f g", o=1).broadcast_to([P, 4, FU + FI, G]),
                    is_at[:, r:r + 4, :].rearrange("p r (o g) -> p r o g", o=1).broadcast_to([P, 4, FU + FI, G]),
                    ALU.mult))
                chain(dve.tensor_reduce(x_all[:, r + 1:r + 5, X_UD:X_POOL], dense_pick[:, :, :, :], AX.X, ALU.add))
            dve.wait_ge(weights_loaded, 16 * (N_WEIGHT + 13))
            dve.tensor_tensor(w_hist[:, :], w_hist[:, :], w_diff[:, :], ALU.add)
            dve.tensor_scalar(w_item[D:P, :], w_item[D:P, :], -1.0, None, ALU.mult)
            chain(dve.tensor_tensor(w_tmp[:, :], w_item[0:D, 0:D], w_diff_lo[:, :], ALU.subtract))
            dve.scalar_tensor_tensor(out=w_last[:, :], in0=w_prod[0:D, 0:D], scalar=last_col[:, :],
                                     in1=w_tmp[:, :], op0=ALU.mult, op1=ALU.add).then_inc(w_ready, 1)
            for r in range(G // 4):
                dve.wait_ge(setup_act, 3 * r + 2)
                dve.tensor_copy(itemT[D:P, r * N:(r + 1) * N], psT[0:D, :]).then_inc(w_ready, 1)
            dve.wait_ge(setup_pe, 4 * (G // 4) + 3)
            chain(dve.tensor_scalar(last_score[:, 0:G], psS[:, 16:16 + G], b2[:, :], None, ALU.add))

            with dve.Fori(0, 1) as z:
                start_score(z, z + (FIRST + PREP + 4))
            dve.sem_inc(scores_read, 1)
            dve.sem_inc(pooled, 1)
            dve.wait_ge(hist_gathered, 16 * (G - 1))

            def times_item(g, t):
                item = itemT[:, bass.ds(g * P, P)].rearrange("p (o n) -> p o n", o=1).broadcast_to([P, PAIRS, P])
                dve.wait_ge(hT_ready, t + 1)
                dve.tensor_tensor(pT[:, :].rearrange("p (q n) -> p q n", q=PAIRS),
                                  psT[:, :].rearrange("p (q n) -> p q n", q=PAIRS), item, ALU.mult
                                  ).then_inc(pT_ready, 1)

            def sum_before(t, half, other):
                dve.wait_ge(weighted, t + 1)
                dve.wait_ge(copied, t * 2 + 4)
                dve.wait_ge(pooled, t + 1)
                dve.tensor_tensor(prod[:, :, :],
                                  rows_x[:, bass.ds(other, 1), :, :].rearrange("p o j f -> p (o j) f"),
                                  e9[:, :].rearrange("p (j o) -> p j o", o=1).broadcast_to([P, SLOTS + 1, AW]),
                                  ALU.mult).then_inc(soft_step, 1)
                dve.wait_ge(soft_step, t * 3 + 1)
                dve.tensor_reduce(rows_x[:, bass.ds(half, 1), SLOTS, :].rearrange("p o f -> p (o f)"),
                                  prod[:, :, :].rearrange("p j f -> p f j"), AX.X, ALU.add).then_inc(pooled, 1)

            def softmax(t):
                flat = bass.ds(t * SLOTS, SLOTS)
                dve.wait_ge(scored, t + 1)
                dve.scalar_tensor_tensor(out=score9[:, 0:SLOTS], in0=psS[:, 0:SLOTS], scalar=b2[:, :],
                                         in1=keep_all[:, flat], op0=ALU.add, op1=ALU.mult
                                         ).then_inc(scores_read, 1)
                dve.wait_ge(scores_read, t + 2)
                dve.tensor_tensor(score9[:, 0:SLOTS], score9[:, 0:SLOTS], pen_all[:, flat], ALU.add
                                  ).then_inc(soft_step, 1)
                dve.wait_ge(soft_step, t * 3 + 3)
                dve.tensor_reduce(neg_max[:, :], score9[:, :], AX.X, ALU.max, negate=True).then_inc(masked, 1)

            def finish(slot, half, t, n0):
                acc = rows_x[:, bass.ds(half, 1), SLOTS, :].rearrange("p o f -> p (o f)")
                dve.wait_ge(pooled, t + 2)
                dve.reciprocal(inv_sum[:, :], acc[:, D:AW]).then_inc(fin_step, 1)
                dve.wait_ge(fin_step, n0 + 1)
                dst = x_all[:, slot, X_POOL:XW] if isinstance(slot, int) else \
                    x_all[:, bass.ds(slot, 1), X_POOL:XW].rearrange("p o f -> p (o f)")
                dve.tensor_scalar(dst, acc[:, 0:D], inv_sum[:, :], None, ALU.mult).then_inc(x_ready, 1)
                return acc

            with dve.Fori(0, G) as g:
                chunks, before = load_plan(dve, g)
                next_chunks = dve.value_load(plan[0:1, bass.ds(g + 1, 1)], min_val=1, max_val=MAXC)
                next_before = dve.value_load(plan[0:1, bass.ds(g + 33, 1)], min_val=0, max_val=G * MAXC)
                steps = (g + 1) * PER_GROUP + FIRST
                times_item(g, before)
                start = dve.compute_val(dve.snap(before % 2))
                sum_before(before, start, dve.compute_val(dve.snap((before + 1) % 2)))
                acc = finish(g, start, before, g * 2)
                dve.tensor_scalar(score9[:, SLOTS:SLOTS + 1], last_start[:, bass.ds(g, 1)], 1.0, None, ALU.mult
                                  ).then_inc(soft_step, 1)
                dve.wait_ge(x_ready, g + 1)
                dve.tensor_scalar(acc, last_row[:, :], n_last[:, bass.ds(g, 1)], None, ALU.mult).then_inc(fin_step, 1)
                prepare(g + 1, steps)
                dve.wait_ge(fin_step, g * 2 + 2)
                dve.wait_ge(prep_step, steps + PREP)
                dve.sem_inc(sorting, 1)
                sort_step(next_before + 0)
                softmax(before)
                with dve.Fori(1, chunks) as c:
                    t = dve.snap(before + c)
                    half = dve.compute_val(dve.snap(t % 2))
                    other = dve.compute_val(dve.snap((t + 1) % 2))
                    times_item(g, t)
                    sum_before(t, half, other)
                    dve.tensor_scalar(score9[:, SLOTS:SLOTS + 1], neg_max[:, :], -1.0, None, ALU.mult
                                      ).then_inc(soft_step, 1)
                    with dve.If(c < next_chunks):
                        sort_step(next_before + c)
                    softmax(t)
                with dve.If(chunks < next_chunks):
                    with dve.Fori(chunks, next_chunks) as c:
                        sort_step(next_before + c)
                masks(next_before, steps + PREP, next_before + next_chunks)
                start_score(g + 1, steps + PREP + 4)
            with dve.Fori(0, 1) as z:
                total = dve.value_load(plan[0:1, bass.ds(z + (32 + G), 1)], min_val=G * MIN_CHUNKS, max_val=G * MAXC)
                half = dve.compute_val(dve.snap(total % 2))
                sum_before(total, half, dve.compute_val(dve.snap((total + 1) % 2)))
                finish(G, half, total, z + G * 2)
            dve.wait_ge(probs_ready, 1)
            chain(dve.tensor_tensor(
                probs_pick[:, :, :], is_at[:, :, :].rearrange("p r g -> p g r"),
                probs[:, :].rearrange("p (o r) -> p o r", o=1).broadcast_to([P, G, G]), ALU.mult))
            dve.tensor_reduce(probs_nat[:, :], probs_pick[:, :, :], AX.X, ALU.add).then_inc(probs_ready, 1)


_NAMES = {
    "user_dense": "r_user_dense", "user_id": "r_user_id", "item_id": "r_item_id",
    "item_category": "r_item_category", "item_dur_bkt": "r_item_dur_bkt", "item_dense": "r_item_dense",
    "history": "r_history_seq",
} | {n: f"L0_rec_{n}" for n in (
    "user_W", "item_W", "cat_W", "dur_W", "hist_W", "aW0", "ab0", "aW1", "ab1", "aW2", "ab2",
    "mW0", "mb0", "mW1", "mb1", "mW2", "mb2")}


def kernel(**inputs):
    import numpy as np
    import concourse.bacc as bacc
    from concourse.bass_utils import run_bass_kernel_spmd

    nc = bacc.Bacc("TRN2", target_bir_lowering=False, num_devices=1)
    arrays = {k: np.ascontiguousarray(inputs[name]) for k, name in _NAMES.items()}
    groups = arrays["history"].shape[0] // P
    arrays["ident"] = np.eye(P, dtype=np.float32)
    arrays["scan"] = np.concatenate(
        [np.eye(groups, dtype=np.float32), np.triu(np.ones((groups, groups + 1), np.float32), 1)], axis=1)
    lanes = np.tile(np.arange(groups + 1, dtype=np.float32), (P, 1))
    lanes[:, groups] = np.arange(P) * groups
    arrays["lanes"] = lanes
    args = {k: nc.dram_tensor(f"in_{k}", v.shape, mybir.dt.from_np(v.dtype), kind="ExternalInput").ap()
            for k, v in arrays.items()}
    out = nc.dram_tensor("out_y", [arrays["history"].shape[0]], F32, kind="ExternalOutput").ap()
    build(nc, args, out)
    r = run_bass_kernel_spmd(nc, [{f"in_{k}": v for k, v in arrays.items()}], core_ids=[0])
    return np.asarray(r.results[0]["out_y"])
```

```python
from contextlib import ExitStack

import concourse.bass as bass
from concourse import mybir

F32 = mybir.dt.float32
I32 = mybir.dt.int32
ALU = mybir.AluOpType
ACT = mybir.ActivationFunctionType
AX = mybir.AxisListType

P = 128
SLOTS = 8
PAIRS = SLOTS // 2
MASKED = -1.0e9
ABSENT = -3.0e9
DEPTH = 4
MIN_CHUNKS = DEPTH + 1
PAD_KEY = 0.25


def build(nc, a, out):
    B, L = a["history"].shape
    LAST = a["hist_W"].shape[0] - 1
    D = a["hist_W"].shape[1]
    G = B // P
    MAXC = L // SLOTS
    T = G * MAXC + DEPTH
    LAST_KEY = -(LAST + 1.0)
    DUMMY = 2
    NK = (G * MAXC + MAXC) * SLOTS
    NU, NI = a["user_W"].shape[0], a["item_W"].shape[0]
    NC_, DC = a["cat_W"].shape
    ND, DD = a["dur_W"].shape
    H1, H2 = a["aW1"].shape
    FU, FI = a["user_dense"].shape[1], a["item_dense"].shape[1]
    M0, M1 = a["mW1"].shape
    X_USER, X_ITEM, X_UD = 0, D, 2 * D
    M_CAT, M_UD = 2 * D, 2 * D + DC + DD
    X_ID = X_UD + FU
    X_POOL = X_ID + FI
    XW = X_POOL + D
    XB = XW - P
    NV = -(-NC_ // P)
    KC = NC_ // NV
    CD = 32
    BF16 = mybir.dt.bfloat16
    N = PAIRS * P
    AW = D + 1
    assert NC_ % NV == 0 and ND <= P and DC + DD <= CD
    assert B % P == 0 and G % 4 == 0 and L % SLOTS == 0 and 2 * D == P and 4 * H2 == P and M0 == 2 * P and M1 == P

    ctx = ExitStack()
    with ctx:
        def sb(name, shape, dt=F32):
            return ctx.enter_context(nc.sbuf_tensor(name, shape, dt))

        def psum(name, shape):
            return ctx.enter_context(nc.psum_tensor(name, shape, F32))

        def sem(name):
            return ctx.enter_context(nc.semaphore(name))

        hist_nat = sb("hist_nat", [P, G, L], I32)
        hist_ids = sb("hist_ids", [P, G + 1, L], I32)
        raw_ids = sb("raw_ids", [P, 4, G], I32)
        row_nat = sb("row_nat", [P, 4, G])
        rank_rows = sb("rank_rows", [P, 4, G])
        row_ids = sb("row_ids", [P, 4, G], I32)
        starts = sb("starts", [G, T])
        before_slots = sb("before_slots", [G, 1])
        end_slot = sb("end_slot", [G, 1])
        in_group = sb("in_group", [G, T])
        in_later = sb("in_later", [G, T])
        ones = sb("ones", [G, 1])
        slots_of = sb("slots_of", [1, T], I32)
        sums = [sb(f"sums{k}", [1, T]) for k in range(2)]
        gathers_to = sb("gathers_to", [1, T], I32)
        lanes = sb("lanes", [P, G + 1])
        rank_key = sb("rank_key", [P, G])
        rank_left = sb("rank_left", [P, G])
        ranked = sb("ranked", [P, G])
        ranked_i = sb("ranked_i", [P, G], I32)
        count_i = sb("count_i", [P, G], I32)
        rank_count = sb("rank_count", [P, G])
        place_i = sb("place_i", [P, G], I32)
        hist_row = sb("hist_row", [P, G], I32)
        is_at = sb("is_at", [P, G, G])
        picked = sb("picked", [P, 4, G, G])
        dense_nat = sb("dense_nat", [P, G, FU + FI])
        dense_pick = sb("dense_pick", [P, FU + FI, G])
        probs_pick = sb("probs_pick", [P, G, G])
        probs_nat = sb("probs_nat", [P, G])
        wrap_ids = sb("wrap_ids", [P, 4, G])
        scratch = sb("scratch", [P, max(G * L, 2 * G * P)])
        in_range = scratch[:, 0:G * L].rearrange("p (g l) -> p g l", g=G)
        wide = scratch[:, 0:2 * G * P].rearrange("p (k b) -> p k b", k=2)
        row_count = sb("row_count", [P, G])
        max_col = sb("max_col", [G, 1])
        chunks_i = sb("chunks_i", [G, 1], I32)
        chunks_i2 = sb("chunks_i2", [G, 1], I32)
        chunks_f = sb("chunks_f", [G, 1])
        plan = sb("plan", [1, 96], I32)
        ident = sb("ident", [P, P])
        scan = sb("scan", [G, 2 * G + 1])
        key = sb("key", [P, L])
        key_wrap = sb("key_wrap", [P, L])
        key_row = sb("key_row", [P, L])
        top8 = sb("top8", [P, SLOTS])
        rows_all = sb("rows_all", [P, NK], I32)
        vals_all = sb("vals_all", [P, NK])
        keep_all = sb("keep_all", [P, NK])
        pen_all = sb("pen_all", [P, NK])
        pen_pad = sb("pen_pad", [P, L])
        n_last = sb("n_last", [P, G + 1])
        has_last = sb("has_last", [P, 1])
        has_pen = sb("has_pen", [P, 1])
        last_kept = sb("last_kept", [P, 1])
        last_start = sb("last_start", [P, G + 1])
        last_score = sb("last_score", [P, G + 1])
        idx = [sb(f"idx{p}", [P, SLOTS], I32) for p in range(DEPTH)]
        hist_in = sb("hist_in", [P, DEPTH, SLOTS, D])
        hist_pe = sb("hist_pe", [P, SLOTS * D])
        rows_x = sb("rows_x", [P, 2, SLOTS + 1, AW])
        hT = sb("hT", [P, N])
        pT = sb("pT", [P, N])
        h1 = sb("h1", [P, N])
        h2 = sb("h2", [P, N // 2])
        score9 = sb("score9", [P, SLOTS + 1])
        neg_max = sb("neg_max", [P, 1])
        e9 = sb("e9", [P, SLOTS + 1])
        prod = sb("prod", [P, SLOTS + 1, AW])
        inv_sum = sb("inv_sum", [P, 1])
        itemT = sb("itemT", [P, (G + 1) * P])
        x_all = sb("x_all", [P, G + 1, XW])
        x_pe = sb("x_pe", [P, XW])
        xT = sb("xT", [P, 2 * P])
        m0 = sb("m0", [P, 2 * P])
        m1 = sb("m1", [P, P])
        logits = sb("logits", [P, G + 1])
        warm = sb("warm", [P, 1])
        probs = sb("probs", [P, G])
        w_hist = sb("w_hist", [P, P])
        w_diff = sb("w_diff", [P, P])
        w_prod = sb("w_prod", [P, P])
        w_item = sb("w_item", [P, P])
        w_last = sb("w_last", [D, H1])
        w_tmp = sb("w_tmp", [D, H1])
        w_diff_lo = sb("w_diff_lo", [D, H1])
        last_col = sb("last_col", [D, 1])
        last_row = sb("last_row", [P, AW])
        bias_last = sb("bias_last", [D, 1])
        w1 = sb("w1", [P, 2 * H2])
        w2 = sb("w2", [P, 4])
        b0 = sb("b0", [P, 1])
        b1 = sb("b1", [P, 1])
        b2 = sb("b2", [P, 1])
        hl1 = sb("hl1", [D, 2, N])
        hl2 = sb("hl2", [H2, 2, N])
        vocab = sb("vocab", [P, NV + 1])
        tab = sb("tab", [P, NV + 1, CD])
        tab_parts = sb("tab_parts", [P, NV + 1, 3 * CD], BF16)
        tab_part = sb("tab_part", [P, NV + 1, CD])
        tab_rest = sb("tab_rest", [P, NV + 1, CD])
        hot = sb("hot", [P, NV + 1, P], BF16)
        cd_T = sb("cd_T", [3 * CD, P])
        mw_cd = sb("mw_cd", [3 * CD, M0])
        mw0 = sb("mw0", [P, 2, M0])
        mw1 = sb("mw1", [P, 2, M1])
        mw2 = sb("mw2", [P, 1])
        mb0 = sb("mb0", [P, 2])
        mb1 = sb("mb1", [P, 1])
        mb2 = sb("mb2", [P, 1])

        psT = psum("psT", [P, 512])
        psL1 = psum("psL1", [P, 512])
        psL2 = psum("psL2", [P, 512])
        psS = psum("psS", [P, 512])
        psX = psum("psX", [P, 512])
        psM0 = psum("psM0", [P, 512])
        psM1 = psum("psM1", [P, 512])
        psY = psum("psY", [P, 512])

        ids_loaded = sem("ids_loaded")
        hist_loaded = [sem(f"hist_loaded{k}") for k in range(4)]
        slots_ready = sem("slots_ready")
        slots_summed = sem("slots_summed")
        counts_ready = sem("counts_ready")
        chunks_ready = sem("chunks_ready")
        ranks_ready = sem("ranks_ready")
        hist0_gathered = sem("hist0_gathered")
        hist_gathered = sem("hist_gathered")
        consts_loaded = sem("consts_loaded")
        weights_loaded = sem("weights_loaded")
        dense_loaded = sem("dense_loaded")
        zeroed = sem("zeroed")
        pool_zeroed = sem("pool_zeroed")
        ids_ready = sem("ids_ready")
        emb_gathered = sem("emb_gathered")
        side_gathered = sem("side_gathered")
        setup_dve = sem("setup_dve")
        setup_pe = sem("setup_pe")
        bias_read = sem("bias_read")
        item_turned = sem("item_turned")
        item_kept = sem("item_kept")
        item_low = sem("item_low")
        last_l1 = sem("last_l1")
        last_h1 = sem("last_h1")
        last_l2 = sem("last_l2")
        last_h2 = sem("last_h2")
        last_l3 = sem("last_l3")
        tables_loaded = sem("tables_loaded")
        mlp_loaded = sem("mlp_loaded")
        ids_wide = sem("ids_wide")
        wide_kept = sem("wide_kept")
        hot_ready = sem("hot_ready")
        dense_step = sem("dense_step")
        plan_ready = sem("plan_ready")
        w_ready = sem("w_ready")
        sorted_ = sem("sorted_")
        sorting = sem("sorting")
        sort_chain = sem("sort_chain")
        prep_step = sem("prep_step")
        fin_step = sem("fin_step")
        soft_step = sem("soft_step")
        idx_loaded = [sem(f"idx_loaded{p}") for p in range(DEPTH)]
        gathered = [sem(f"gathered{p}") for p in range(DEPTH)]
        begun = sem("begun")
        landed = sem("landed")
        copied = sem("copied")
        transposed = sem("transposed")
        hT_ready = sem("hT_ready")
        pT_ready = sem("pT_ready")
        l1_done = sem("l1_done")
        h1_ready = sem("h1_ready")
        l2_done = sem("l2_done")
        h2_ready = sem("h2_ready")
        scored = sem("scored")
        scores_read = sem("scores_read")
        masked = sem("masked")
        weighted = sem("weighted")
        pooled = sem("pooled")
        x_ready = sem("x_ready")
        x_copied = sem("x_copied")
        xT_done = sem("xT_done")
        xT_ready = sem("xT_ready")
        m0_done = sem("m0_done")
        m0_ready = sem("m0_ready")
        m1_done = sem("m1_done")
        m1_ready = sem("m1_ready")
        y_done = sem("y_done")
        y_read = sem("y_read")
        probs_ready = sem("probs_ready")
        stored = sem("stored")

        def grouped(ap):
            return ap.rearrange("(p g) f -> p g f", g=G)

        def load_chunks(eng, g):
            return eng.value_load(plan[0:1, bass.ds(g, 1)], min_val=MIN_CHUNKS, max_val=MAXC)

        def load_last(eng, g):
            return eng.value_load(plan[0:1, bass.ds(g + 64, 1)], min_val=MIN_CHUNKS - 1, max_val=MAXC - 1)

        def load_before(eng, g):
            return eng.value_load(plan[0:1, bass.ds(g + 32, 1)], min_val=0, max_val=G * MAXC)

        turned = (psT, psX, psM0, psM1)
        last_ps = (psL1, psY)

        def m0_halves(last):
            return psM0[:, 0:P], psL2[:, 0:P] if last else psM0[:, P:2 * P]

        block = ctx.enter_context(nc.Block())
        N_CONST, N_WEIGHT, N_DENSE, N_TABLE, N_MLP = 4, 22, 2, 3, 12

        @block.sync
        def _(sp):
            for k in range(4):
                part = slice(k * (G // 4), (k + 1) * (G // 4))
                sp.dma_start(hist_nat[:, part, :], grouped(a["history"])[:, part, :]).then_inc(hist_loaded[k], 16)
            sp.dma_start(lanes[:, :], a["lanes"]).then_inc(consts_loaded, 16)
            sp.dma_start(ident[:, :], a["ident"]).then_inc(consts_loaded, 16)
            sp.dma_start(scan[:, :], a["scan"]).then_inc(consts_loaded, 16)
            sp.dma_start(starts[:, :], a["starts"]).then_inc(consts_loaded, 16)
            sp.dma_start(vocab[:, :], a["vocab"]).then_inc(tables_loaded, 16)
            sp.dma_start(dense_nat[:, :, 0:FU], grouped(a["user_dense"])).then_inc(dense_loaded, 16)
            sp.dma_start(dense_nat[:, :, FU:FU + FI], grouped(a["item_dense"])).then_inc(dense_loaded, 16)

            sp.wait_ge(slots_ready, 3)
            total = sp.value_load(plan[0:1, 32 + G:33 + G], min_val=G * MIN_CHUNKS, max_val=G * MAXC)
            rounds = sp.snap((total + (DEPTH - 1)) // DEPTH)
            for p in range(DEPTH):
                sp.wait_ge(sorted_, p + 1)
                sp.dma_start(idx[p][:, :], rows_all[:, p * SLOTS:(p + 1) * SLOTS]).then_inc(idx_loaded[p], 16)
            with sp.Fori(0, rounds) as i:
                for p in range(DEPTH):
                    count = sp.value_load(gathers_to[0:1, bass.ds(i * DEPTH + p, 1)], min_val=1, max_val=T * SLOTS)
                    sp.wait_ge(gathered[p], count * 16)
                    sp.sem_inc(landed, 1)
                    sp.wait_ge(sorted_, i * DEPTH + (DEPTH + 1 + p))
                    sp.dma_start(idx[p][:, :],
                                 rows_all[:, bass.ds(i * (DEPTH * SLOTS) + (DEPTH + p) * SLOTS, SLOTS)]
                                 ).then_inc(idx_loaded[p], 16)
            sp.sem_inc(landed, 1)
            last = sp.snap(rounds * 16 + 16)
            for p in range(DEPTH):
                sp.wait_ge(idx_loaded[p], last)
            sp.wait_ge(probs_ready, 2)
            sp.dma_start(out.rearrange("(p g) -> p g", g=G), probs_nat[:, :]).then_inc(stored, 16)
            sp.wait_ge(stored, 16)

        @block.gpsimd
        def _(pool):
            def rows(table, ids, dst):
                return pool.indirect_dma_start(
                    out=dst, out_offset=None, in_=table, in_offset=bass.IndirectOffsetOnAxis(ap=ids, axis=0))

            def slot_row(p, j):
                rows(a["hist_W"], idx[p][:, j:j + 1], hist_in[:, p, j, :]).then_inc(gathered[p], 16)

            pool.memset(vals_all[:, :], LAST_KEY)
            pool.memset(rows_x[:, :, :, :], 1.0)
            pool.memset(hist_in[:, :, :, :], 0.0)
            pool.memset(rows_all[:, :], LAST)
            pool.memset(hist_ids[:, G, :], LAST).then_inc(pool_zeroed, 1)
            pool.wait_ge(pool_zeroed, 1)

            pool.wait_ge(ranks_ready, 1)
            EARLY = 4

            def history(g):
                rows(a["history"], hist_row[:, g:g + 1], hist_ids[:, g, :]
                     ).then_inc(hist_gathered if g else hist0_gathered, 16)

            for g in range(EARLY):
                history(g)
            pool.wait_ge(ids_ready, 1)
            for g in range(G):
                rows(a["item_W"], row_ids[:, 1, g:g + 1], x_all[:, g + 1, X_ITEM:X_ITEM + D]).then_inc(emb_gathered, 16)
            for g in range(EARLY, G):
                history(g)
            for g in range(G):
                rows(a["user_W"], row_ids[:, 0, g:g + 1], x_all[:, g + 1, X_USER:X_USER + D]).then_inc(side_gathered, 16)
            pool.wait_ge(plan_ready, 1)
            pool.wait_ge(zeroed, 1)
            pool.wait_ge(slots_ready, 2)
            total = pool.value_load(plan[0:1, 32 + G:33 + G], min_val=G * MIN_CHUNKS, max_val=G * MAXC)
            with pool.Fori(0, pool.snap((total + (DEPTH - 1)) // DEPTH)) as i:
                for p in range(DEPTH):
                    pool.wait_ge(idx_loaded[p], (i + 1) * 16)
                    pool.wait_ge(copied, i * (2 * DEPTH) + (2 * p + 2))
                    pool.sem_inc(begun, 1)
                    used = pool.value_load(slots_of[0:1, bass.ds(i * DEPTH + p, 1)], min_val=1, max_val=SLOTS)
                    slot_row(p, 0)
                    with pool.If(used > SLOTS - 1):
                        for j in range(1, SLOTS):
                            slot_row(p, j)
                    with pool.Else():
                        for j in range(1, SLOTS - 1):
                            with pool.If(used > j):
                                slot_row(p, j)

        @block.scalar
        def _(act):
            wt = a["aW0"]
            Wh, Wt, Wp, Wd = (wt[k * D:(k + 1) * D, :] for k in range(4))
            for k, name in enumerate(("user_id", "item_id", "item_category", "item_dur_bkt")):
                act.dma_start(raw_ids[:, k, :], a[name].rearrange("(p g) -> p g", g=G)).then_inc(ids_loaded, 16)
            act.wait_ge(zeroed, 1)
            n = 0

            def load(dst, src):
                act.dma_start(dst, src).then_inc(weights_loaded, 16)
                return 1

            for h in range(2):
                lo, hi = h * D, (h + 1) * D
                n += load(w_hist[lo:hi, lo:hi], Wh)
                n += load(w_diff[lo:hi, lo:hi], Wd)
                n += load(w_prod[lo:hi, lo:hi], Wp)
                n += load(w_item[0:D, lo:hi], Wt)
                n += load(w_item[D:P, lo:hi], Wd)
                n += load(w1[lo:hi, h * H2:(h + 1) * H2], a["aW1"])
                n += load(b0[lo:hi, :], a["ab0"].rearrange("(f o) -> f o", o=1))
            for q in range(4):
                n += load(w2[q * H2:(q + 1) * H2, q:q + 1], a["aW2"])
                n += load(b1[q * H2:(q + 1) * H2, :], a["ab1"].rearrange("(f o) -> f o", o=1))
            assert n == N_WEIGHT
            n += load(b2[:, :], a["ab2"].rearrange("(o f) -> o f", o=1).broadcast_to([P, 1]))
            n += load(w_diff_lo[:, :], Wd)
            n += load(last_col[:, :], a["hist_W"][LAST:LAST + 1, :].rearrange("o f -> f o"))
            n += load(last_row[:, 0:D], a["hist_W"][LAST:LAST + 1, :].broadcast_to([P, D]))
            assert n == N_WEIGHT + 4
            act.dma_start(tab[0:KC, 0:NV, 0:DC], a["cat_W"].rearrange("(k p) f -> p k f", p=KC)
                          ).then_inc(tables_loaded, 16)
            act.dma_start(tab[0:ND, NV, DC:DC + DD], a["dur_W"]).then_inc(tables_loaded, 16)
            mlp_loads = [(mw_cd[k * CD:k * CD + DC + DD, :], a["mW0"][M_CAT:M_UD, :]) for k in range(3)]
            mlp_loads += [(mw0[:, 0, :], a["mW0"][0:P, :]), (mw0[0:XB, 1, :], a["mW0"][M_UD:M_UD + XB, :])]
            for h in range(2):
                mlp_loads += [(mw1[:, h, :], a["mW1"][h * P:(h + 1) * P, :]),
                              (mb0[:, h:h + 1], a["mb0"][h * P:(h + 1) * P].rearrange("(f o) -> f o", o=1))]
            mlp_loads += [(mw2[:, :], a["mW2"]), (mb1[:, :], a["mb1"].rearrange("(f o) -> f o", o=1)),
                          (mb2[:, :], a["mb2"].rearrange("(o f) -> o f", o=1).broadcast_to([P, 1]))]
            for dst, src in mlp_loads:
                act.dma_start(dst, src).then_inc(mlp_loaded, 16)
            assert len(mlp_loads) == N_MLP
            act.sem_inc(copied, 2 * DEPTH)

            act.wait_ge(weights_loaded, 16 * n)
            act.wait_ge(setup_pe, 3)
            act.activation(bias_last[:, :], psM0[0:D, 0:1], ACT.Identity, bias=b0[0:D, :]).then_inc(bias_read, 1)

            def keep_wide(r):
                act.wait_ge(ids_wide, r + 1)
                act.activation(wide[:, 0, r * N:(r + 1) * N], psL1[:, :], ACT.Copy)
                act.activation(wide[:, 1, r * N:(r + 1) * N], psL2[:, :], ACT.Copy).then_inc(wide_kept, 1)

            keep_wide(0)
            keep_wide(1)
            for r in range(G // 4):
                act.wait_ge(item_turned, r + 1)
                act.activation(itemT[0:D, r * N:(r + 1) * N], turned[r][0:D, :], ACT.Copy).then_inc(item_kept, 1)
            for k in range(G // 4 + 1):
                if k < G // 4:
                    act.wait_ge(last_l1, k + 1)
                    if k >= 2:
                        act.wait_ge(last_l2, k - 1)
                    act.activation(hl1[:, k % 2, :], last_ps[k % 2][0:D, :], ACT.Relu, bias=bias_last[:, :]
                                   ).then_inc(last_h1, 1)
                if k >= 1:
                    act.wait_ge(last_l2, k)
                    if k >= 3:
                        act.wait_ge(last_l3, k - 2)
                    act.activation(hl2[:, (k - 1) % 2, :], psL2[0:H2, :], ACT.Relu, bias=b1[0:H2, :]
                                   ).then_inc(last_h2, 1)
            keep_wide(2)
            keep_wide(3)
            act.wait_ge(mlp_loaded, 16 * N_MLP)

            def mlp_parts(slot, g1):
                def rows():
                    act.wait_ge(x_ready, g1)
                    act.wait_ge(dense_step, slot * 2 + 1)
                    act.activation(x_pe[:, :], x_all[:, slot, :] if isinstance(slot, int)
                                   else x_all[:, bass.ds(slot, 1), :].rearrange("p o f -> p (o f)"),
                                   ACT.Copy).then_inc(x_copied, 2)

                def transposed_rows():
                    act.wait_ge(xT_done, g1 * 2)
                    act.activation(xT[:, 0:P], psX[:, 0:P], ACT.Copy)
                    act.activation(xT[0:XB, P:2 * P], psX[0:XB, P:2 * P], ACT.Copy)
                    act.activation(cd_T[:, :], psX[0:3 * CD, 2 * P:3 * P], ACT.Copy).then_inc(xT_ready, 2)

                def layer0():
                    act.wait_ge(m0_done, g1)
                    m0_ps = m0_halves(isinstance(slot, int))
                    act.activation(m0[:, 0:P], m0_ps[0], ACT.Relu, bias=mb0[:, 0:1]).then_inc(m0_ready, 1)
                    act.activation(m0[:, P:2 * P], m0_ps[1], ACT.Relu, bias=mb0[:, 1:2]
                                   ).then_inc(m0_ready, 1)

                def layer1():
                    act.wait_ge(m1_done, g1)
                    act.activation(m1[:, :], psM1[:, 0:P], ACT.Relu, bias=mb1[:, :]).then_inc(m1_ready, 1)

                def logit():
                    act.wait_ge(y_done, g1)
                    dst = logits[:, slot:slot + 1] if isinstance(slot, int) else logits[:, bass.ds(slot, 1)]
                    act.activation(dst, psY[:, 0:1], ACT.Copy).then_inc(y_read, 1)
                return rows, transposed_rows, layer0, layer1, logit

            none = [lambda: None] * 5

            act.sem_inc(weighted, 1)
            act.wait_ge(side_gathered, 16 * G)
            act.wait_ge(pool_zeroed, 1)

            def rows_of(at):
                if isinstance(at, int):
                    return hist_in[:, at, :, :]
                return hist_in[:, bass.ds(at, 1), :, :].rearrange("p o j d -> p (o j) d")

            def copy_hist(at):
                act.activation(hist_pe[:, :].rearrange("p (j d) -> p j d", d=D), rows_of(at), ACT.Copy
                               ).then_inc(copied, 1)

            def copy_rows(at, half):
                dst = rows_x[:, half, 0:SLOTS, 0:D] if isinstance(half, int) else \
                    rows_x[:, bass.ds(half, 1), 0:SLOTS, 0:D].rearrange("p o j d -> p (o j) d")
                act.activation(dst, rows_of(at), ACT.Copy).then_inc(copied, 1)

            act.wait_ge(landed, 1)
            copy_hist(0)
            copy_rows(0, 0)
            act.wait_ge(transposed, 1)
            act.activation(hT[:, :], psT[:, :], ACT.Copy).then_inc(hT_ready, 1)
            def chunk(t, mlp=none):
                rows, transposed_rows, layer0, layer1, logit = mlp
                other = act.snap((t + 1) % 2)
                at = act.snap((t + 1) % DEPTH)
                act.wait_ge(l1_done, t + 1)
                act.activation(h1[:, :], psL1[:, :], ACT.Relu, bias=b0[:, :]).then_inc(h1_ready, 1)
                act.wait_ge(landed, t + 2)
                act.wait_ge(transposed, t + 1)
                copy_hist(at)
                rows()
                act.wait_ge(l2_done, t + 1)
                act.activation(h2[:, :], psL2[:, 0:N // 2], ACT.Relu, bias=b1[:, :]).then_inc(h2_ready, 1)
                act.wait_ge(transposed, t + 2)
                act.activation(hT[:, :], psT[:, :], ACT.Copy).then_inc(hT_ready, 1)
                transposed_rows()
                act.wait_ge(pooled, t + 2)
                copy_rows(at, other)
                act.wait_ge(masked, t + 1)
                act.activation(e9[:, :], score9[:, :], ACT.Exp, bias=neg_max[:, :]).then_inc(weighted, 1)
                layer0()
                layer1()
                logit()

            with act.Fori(0, G) as g:
                before = load_before(act, g)
                chunk(before)
                rows, transposed_rows, layer0, layer1, logit = mlp_parts(g, g + 1)
                chunk(act.snap(before + 1), (rows, transposed_rows, layer0, none[0], none[0]))
                chunk(act.snap(before + 2), (none[0], layer1, none[0], none[0], logit))
                chunks = load_chunks(act, g)
                with act.Fori(3, chunks) as c:
                    chunk(act.snap(before + c))
            act.wait_ge(zeroed, 1)
            act.activation(warm[:, :], logits[:, 0:1], ACT.Sigmoid)
            act.activation(x_pe[:, 0:P], x_all[:, G, 0:P], ACT.Copy).then_inc(x_copied, 1)
            act.wait_ge(xT_done, G * 2 + 1)
            act.activation(xT[:, 0:P], psX[:, 0:P], ACT.Copy)
            act.activation(cd_T[:, :], psX[0:3 * CD, 2 * P:3 * P], ACT.Copy).then_inc(xT_ready, 1)
            act.wait_ge(dense_step, G * 2 + 1)
            act.wait_ge(x_ready, G + 1)
            act.activation(x_pe[:, P:XW], x_all[:, G, P:XW], ACT.Copy).then_inc(x_copied, 1)
            act.wait_ge(xT_done, G * 2 + 2)
            act.activation(xT[0:XB, P:2 * P], psX[0:XB, P:2 * P], ACT.Copy).then_inc(xT_ready, 1)
            for part in mlp_parts(G, G + 1)[2:]:
                part()
            act.wait_ge(y_read, G + 1)
            act.activation(probs[:, :], logits[:, 1:G + 1], ACT.Sigmoid, bias=mb2[:, :]).then_inc(probs_ready, 1)

        @block.tensor
        def _(pe):
            pe.wait_ge(consts_loaded, 16 * N_CONST)
            pe.wait_ge(counts_ready, 1)
            pe.transpose(psX[0:G, 0:P], rank_count[:, :], ident[:, :]).then_inc(setup_pe, 1)
            pe.wait_ge(chunks_ready, 1)
            pe.matmul(psX[0:1, P:P + 2 * G + 1], chunks_f[:, :], scan[:, :], start=True, stop=True
                      )
            pe.matmul(psX[0:G, 2 * P:2 * P + 1], scan[:, G:2 * G], chunks_f[:, :], start=True, stop=True
                      ).then_inc(setup_pe, 1)
            pe.wait_ge(slots_ready, 1)
            pe.matmul(psM1[0:1, 0:T], ones[:, :], in_group[:, :], start=True, stop=True).then_inc(slots_summed, 1)
            pe.wait_ge(w_ready, 1)
            pe.matmul(psM0[0:D, 0:1], w_hist[0:D, 0:D], last_col[:, :], start=True, stop=True
                      ).then_inc(setup_pe, 1)

            def widen(r):
                if r:
                    pe.wait_ge(wide_kept, r)
                for q in range(4):
                    g = 4 * r + q
                    pe.matmul(psL1[:, q * P:(q + 1) * P], rank_rows[:, 2, g:g + 1].broadcast_to([P, P]), ident[:, :],
                              start=True, stop=True)
                    ins = pe.matmul(psL2[:, q * P:(q + 1) * P], rank_rows[:, 3, g:g + 1].broadcast_to([P, P]),
                                    ident[:, :], start=True, stop=True)
                ins.then_inc(ids_wide, 1)

            pe.wait_ge(ids_ready, 1)
            widen(0)
            widen(1)
            pe.wait_ge(emb_gathered, 16 * G)
            pe.wait_ge(bias_read, 1)
            pe.wait_ge(slots_ready, 2)
            for r in range(G // 4):
                for q in range(4):
                    ins = pe.transpose(turned[r][0:D, q * P:(q + 1) * P], x_all[:, 4 * r + q + 1, X_ITEM:X_ITEM + D],
                                       ident[:, :])
                ins.then_inc(item_turned, 1)
            pe.wait_ge(wide_kept, 2)
            for k in range(G // 4 + 2):
                if k < G // 4:
                    pe.wait_ge(item_kept, k + 1)
                    if k >= 2:
                        pe.wait_ge(last_h1, k - 1)
                    pe.matmul(last_ps[k % 2][0:D, :], w_last[:, :], itemT[0:D, k * N:(k + 1) * N],
                              start=True, stop=True).then_inc(last_l1, 1)
                if 0 <= k - 1 < G // 4:
                    pe.wait_ge(last_h1, k)
                    if k >= 2:
                        pe.wait_ge(last_h2, k - 1)
                    pe.matmul(psL2[0:H2, :], w1[0:D, 0:H2], hl1[:, (k - 1) % 2, :], start=True, stop=True
                              ).then_inc(last_l2, 1)
                if k >= 2:
                    pe.wait_ge(last_h2, k - 1)
                    for q in range(4):
                        b = 16 + 4 * (k - 2) + q
                        ins = pe.matmul(psS[:, b:b + 1], hl2[:, (k - 2) % 2, q * P:(q + 1) * P], w2[0:H2, 0:1],
                                        start=True, stop=True)
                    ins.then_inc(last_l3, 1)
            widen(2)
            widen(3)
            pe.wait_ge(item_low, G // 4)
            pe.wait_ge(mlp_loaded, 16 * N_MLP)
            pe.wait_ge(wide_kept, G // 4)

            def transpose_rows():
                for q in range(PAIRS):
                    ins = pe.transpose(psT[:, q * P:(q + 1) * P], hist_pe[:, q * P:(q + 1) * P], ident[:, :])
                ins.then_inc(transposed, 1)

            def mlp_parts(slot, g1):
                def look_up():
                    pe.wait_ge(hot_ready, slot + 1)
                    for k in range(NV + 1):
                        rows = KC if k < NV else ND
                        pe.matmul(psX[0:3 * CD, 2 * P:3 * P], tab_parts[0:rows, k, :], hot[0:rows, k, :],
                                        start=(k == 0), stop=(k == NV))

                m0_ps = m0_halves(isinstance(slot, int))

                def ids_part(h):
                    pe.matmul(m0_ps[h], mw0[:, 0, h * P:(h + 1) * P], xT[:, 0:P], start=True, stop=False)
                    pe.matmul(m0_ps[h], mw_cd[:, h * P:(h + 1) * P], cd_T[:, :], start=False, stop=False)

                def pooled_part(h):
                    return pe.matmul(m0_ps[h], mw0[0:XB, 1, h * P:(h + 1) * P], xT[0:XB, P:2 * P],
                                     start=False, stop=True)

                def rows():
                    look_up()
                    pe.wait_ge(x_copied, g1 * 2)
                    pe.transpose(psX[:, 0:P], x_pe[:, 0:P], ident[:, :])
                    pe.transpose(psX[0:XB, P:2 * P], x_pe[:, P:XW], ident[:, :]).then_inc(xT_done, 2)

                def layer0():
                    pe.wait_ge(xT_ready, g1 * 2)
                    for h in range(2):
                        ids_part(h)
                        ins = pooled_part(h)
                    ins.then_inc(m0_done, 1)

                def layer0_in_two():
                    look_up()
                    pe.wait_ge(x_copied, g1 * 2 - 1)
                    pe.transpose(psX[:, 0:P], x_pe[:, 0:P], ident[:, :]).then_inc(xT_done, 1)
                    pe.wait_ge(xT_ready, g1 * 2 - 1)
                    ids_part(0)
                    ids_part(1)
                    pe.wait_ge(x_copied, g1 * 2)
                    pe.transpose(psX[0:XB, P:2 * P], x_pe[:, P:XW], ident[:, :]).then_inc(xT_done, 1)
                    pe.wait_ge(xT_ready, g1 * 2)
                    pooled_part(0)
                    pooled_part(1).then_inc(m0_done, 1)

                def layer1():
                    for h in range(2):
                        pe.wait_ge(m0_ready, g1 * 2 - 1 + h)
                        ins = pe.matmul(psM1[:, 0:P], mw1[:, h, :], m0[:, h * P:(h + 1) * P],
                                        start=(h == 0), stop=(h == 1))
                    ins.then_inc(m1_done, 1)

                def logit():
                    pe.wait_ge(m1_ready, g1)
                    pe.matmul(psY[:, 0:1], m1[:, :], mw2[:, :], start=True, stop=True).then_inc(y_done, 1)
                if isinstance(slot, int):
                    return layer0_in_two, layer1, logit
                return rows, layer0, layer1, logit

            none = [lambda: None] * 4

            def add_item(g):
                item = itemT[:, bass.ds(g * P, P)].rearrange("p (o n) -> p o n", o=1).broadcast_to([P, PAIRS, P])
                pe.matmul(psL1[:, :].rearrange("p (q n) -> p q n", q=PAIRS), w_item[:, :], item,
                          start=True, stop=False)

            def add_hist(t):
                pe.wait_ge(hT_ready, t + 1)
                pe.matmul(psL1[:, :], w_hist[:, :], hT[:, :], start=False, stop=False)

            def chunk(t, next_g, mlp=none):
                rows, layer0, layer1, logit = mlp
                pe.wait_ge(pT_ready, t + 1)
                pe.matmul(psL1[:, :], w_prod[:, :], pT[:, :], start=False, stop=True).then_inc(l1_done, 1)
                pe.wait_ge(h1_ready, t + 1)
                for u in range(2):
                    ins = pe.matmul(psL2[u * 2 * H2:(u + 1) * 2 * H2, 0:2 * P], w1[:, :],
                                    h1[:, u * 2 * P:(u + 1) * 2 * P], start=True, stop=True)
                ins.then_inc(l2_done, 1)
                pe.wait_ge(copied, t * 2 + (2 * DEPTH + 3))
                transpose_rows()
                rows()
                add_item(next_g)
                pe.wait_ge(h2_ready, t + 1)
                pe.wait_ge(scores_read, t + 1)
                for q in range(2):
                    dst = psS[:, 0:SLOTS].rearrange("p (u q e) -> p u q e", u=2, q=2)[:, :, q, :]
                    ins = pe.matmul(dst, h2[:, q * P:(q + 1) * P],
                                    w2[:, :].rearrange("p (u e) -> p u e", u=2), start=True, stop=True)
                ins.then_inc(scored, 1)
                add_hist(t + 1)
                layer0()
                layer1()
                logit()

            pe.wait_ge(plan_ready, 1)
            pe.wait_ge(copied, 2 * DEPTH + 1)
            transpose_rows()
            with pe.Fori(0, 1) as z:
                add_item(z)
                add_hist(z)
            with pe.Fori(0, G) as g:
                before = load_before(pe, g)
                chunk(before, g)
                rows, layer0, layer1, logit = mlp_parts(g, g + 1)
                chunk(pe.snap(before + 1), g, (rows, layer0, none[0], none[0]))
                chunk(pe.snap(before + 2), g, (layer1, logit, none[0], none[0]))
                last_chunk = load_last(pe, g)
                with pe.Fori(3, last_chunk) as c:
                    chunk(pe.snap(before + c), g)
                chunk(pe.snap(before + last_chunk), g + 1)
            for part in mlp_parts(G, G + 1):
                part()

        @block.vector
        def _(dve):
            step = [0]

            def chain(ins):
                step[0] += 1
                ins.then_inc(setup_dve, 1)
                dve.wait_ge(setup_dve, step[0])

            dve.memset(x_all[:, 0, :], 0.0)
            dve.memset(e9[:, :], 1.0)
            dve.memset(itemT[:, G * P:(G + 1) * P], 0.0)
            dve.memset(ones[:, :], 1.0)
            dve.memset(neg_max[:, :], 0.0)
            for w in (w_hist, w_diff, w_prod, w1, w2, mw_cd):
                dve.memset(w[:, :], 0.0)
            dve.memset(hot[:, :, :], 0.0).then_inc(hot_ready, 1)
            dve.memset(tab[:, :, :], 0.0)
            dve.memset(last_row[:, D:AW], 1.0)
            dve.memset(logits[:, :], 0.0)
            dve.memset(plan[:, :], DUMMY)
            dve.memset(last_score[:, G:G + 1], 0.0).then_inc(zeroed, 1)
            dve.wait_ge(zeroed, 1)

            for k in range(4):
                part = slice(k * (G // 4), (k + 1) * (G // 4))
                dve.wait_ge(hist_loaded[k], 16)
                chain(dve.tensor_scalar(in_range[:, part, :], hist_nat[:, part, :], float(LAST), None, ALU.is_lt))
                ins = dve.tensor_reduce(row_count[:, part], in_range[:, part, :], AX.X, ALU.add)
            chain(ins)
            dve.wait_ge(consts_loaded, 16 * N_CONST)
            chain(dve.scalar_tensor_tensor(out=rank_key[:, :], in0=row_count[:, :], scalar=float(G),
                                           in1=lanes[:, 0:G], op0=ALU.mult, op1=ALU.add))
            chain(dve.max(ranked[:, 0:8], rank_key[:, :]))
            chain(dve.match_replace(rank_left[:, :], ranked[:, 0:8], rank_key[:, :], -1.0))
            chain(dve.max(ranked[:, 8:16], rank_left[:, :]))
            chain(dve.tensor_copy(ranked_i[:, :], ranked[:, :]))
            dve.tensor_scalar(count_i[:, :], ranked_i[:, :], G.bit_length() - 1, None, ALU.logical_shift_right)
            chain(dve.tensor_scalar(place_i[:, :], ranked_i[:, :], G - 1, None, ALU.bitwise_and))
            dve.tensor_copy(rank_count[:, :], count_i[:, :]).then_inc(counts_ready, 1)
            dve.tensor_scalar(hist_row[:, :], place_i[:, :], lanes[:, G:G + 1], None, ALU.add
                              ).then_inc(ranks_ready, 1)
            dve.wait_ge(ids_loaded, 64)
            sizes = (NU, NI, NC_, ND)
            for k in range(4):
                ins = dve.tensor_scalar(wrap_ids[:, k, :], raw_ids[:, k, :], 0.0, float(sizes[k]), ALU.is_lt, ALU.mult)
            chain(ins)
            chain(dve.tensor_tensor(wrap_ids[:, :, :], wrap_ids[:, :, :], raw_ids[:, :, :], ALU.add))
            for k in range(4):
                ins = dve.tensor_scalar(row_nat[:, k, :], wrap_ids[:, k, :], 0.0, float(sizes[k] - 1), ALU.max, ALU.min)
            chain(ins)
            chain(dve.tensor_tensor(
                is_at[:, :, :], ranked[:, :].rearrange("p (r o) -> p r o", o=1).broadcast_to([P, G, G]),
                rank_key[:, :].rearrange("p (o g) -> p o g", o=1).broadcast_to([P, G, G]), ALU.is_equal))
            for k in range(4):
                ins = dve.tensor_tensor(
                    picked[:, k, :, :], is_at[:, :, :],
                    row_nat[:, k, :].rearrange("p (o g) -> p o g", o=1).broadcast_to([P, G, G]), ALU.mult)
            chain(ins)
            chain(dve.tensor_reduce(rank_rows[:, :, :], picked[:, :, :, :], AX.X, ALU.add))
            dve.tensor_copy(row_ids[:, :, :], rank_rows[:, :, :]).then_inc(ids_ready, 1)
            dve.wait_ge(setup_pe, 1)
            chain(dve.tensor_reduce(max_col[:, :], psX[0:G, 0:P], AX.X, ALU.max))
            chain(dve.tensor_scalar(chunks_i[:, :], max_col[:, :], float(SLOTS - 1), None, ALU.add))
            chain(dve.tensor_scalar(chunks_i2[:, :], chunks_i[:, :], SLOTS.bit_length() - 1, None,
                                    ALU.logical_shift_right))
            dve.tensor_scalar(chunks_f[:, :], chunks_i2[:, :], float(MIN_CHUNKS), None, ALU.max
                              ).then_inc(chunks_ready, 1)
            dve.wait_ge(setup_pe, 2)
            chain(dve.tensor_copy(plan[:, 0:G], psX[0:1, P:P + G]))
            chain(dve.tensor_scalar(plan[:, 64:64 + G], psX[0:1, P:P + G], -1.0, None, ALU.add))
            dve.tensor_copy(plan[:, 32:33 + G], psX[0:1, P + G:P + 2 * G + 1]).then_inc(plan_ready, 1)
            dve.wait_ge(plan_ready, 1)
            chain(dve.tensor_scalar(before_slots[:, :], psX[0:G, 2 * P:2 * P + 1], float(SLOTS), None, ALU.mult))
            chain(dve.tensor_tensor(end_slot[:, :], before_slots[:, :], max_col[:, :], ALU.add))
            dve.tensor_scalar(in_group[:, :], starts[:, :], end_slot[:, :], -1.0, ALU.subtract, ALU.mult)
            chain(dve.tensor_scalar(in_later[:, :], starts[:, :], before_slots[:, :], -float(SLOTS), ALU.is_lt, ALU.mult))
            chain(dve.tensor_scalar(in_group[:, :], in_group[:, :], 0.0, float(SLOTS), ALU.max, ALU.min))
            dve.tensor_tensor(in_group[:, :], in_group[:, :], in_later[:, :], ALU.add).then_inc(slots_ready, 1)
            dve.wait_ge(slots_summed, 1)
            chain(dve.tensor_scalar(slots_of[:, :], psM1[0:1, 0:T], 1.0, None, ALU.max))
            dve.sem_inc(slots_ready, 1)

            PREP = 8

            def prepare(g, n0):
                ids = hist_ids[:, bass.ds(g, 1), :].rearrange("p o l -> p (o l)")
                dve.wait_ge(prep_step, n0)
                dve.tensor_scalar(key_wrap[:, :], ids, 0.0, float(LAST + 1), ALU.is_lt, ALU.mult
                                  ).then_inc(prep_step, 1)
                dve.wait_ge(prep_step, n0 + 1)
                dve.tensor_tensor(key_row[:, :], ids, key_wrap[:, :], ALU.add).then_inc(prep_step, 1)
                dve.wait_ge(prep_step, n0 + 2)
                dve.tensor_scalar(key_wrap[:, :], key_row[:, :], 0.0, float(LAST), ALU.max, ALU.min
                                  ).then_inc(prep_step, 1)
                dve.wait_ge(prep_step, n0 + 3)
                dve.tensor_scalar(key_row[:, :], key_wrap[:, :], -1.0, -1.0, ALU.mult, ALU.add
                                  ).then_inc(prep_step, 1)
                dve.tensor_scalar(pen_pad[:, :], ids, 0.0, PAD_KEY, ALU.is_equal, ALU.mult
                                  ).then_inc(prep_step, 1)
                dve.wait_ge(prep_step, n0 + 5)
                dve.tensor_tensor(key[:, :], key_row[:, :], pen_pad[:, :], ALU.add).then_inc(prep_step, 1)
                dve.wait_ge(prep_step, n0 + 6)
                dve.tensor_scalar(key_row[:, :], key[:, :], LAST_KEY, None, ALU.is_le).then_inc(prep_step, 1)
                dve.wait_ge(prep_step, n0 + 7)
                dve.tensor_reduce(n_last[:, bass.ds(g, 1)], key_row[:, :], AX.X, ALU.add).then_inc(prep_step, 1)

            def sort_step(k):
                flat = bass.ds(k * SLOTS, SLOTS)
                dve.max(top8[:, :], key[:, :]).then_inc(sort_chain, 1)
                dve.wait_ge(sort_chain, k * 3 + 1)
                dve.tensor_scalar(rows_all[:, flat], top8[:, :], -1.0, -1.0, ALU.mult, ALU.add
                                  ).then_inc(sorted_, 1)
                dve.tensor_scalar(vals_all[:, flat], top8[:, :], 1.0, None, ALU.mult).then_inc(sort_chain, 1)
                dve.match_replace(key[:, :], top8[:, :], key[:, :], LAST_KEY).then_inc(sort_chain, 1)
                dve.wait_ge(sort_chain, k * 3 + 3)
                dve.sem_inc(sorting, 1)

            def masks(before, n0, k_end):
                span = bass.ds(before * SLOTS, L)
                dve.wait_ge(sort_chain, k_end * 3)
                dve.tensor_scalar(pen_all[:, span], vals_all[:, span], LAST_KEY, ABSENT, ALU.is_le, ALU.mult
                                  ).then_inc(prep_step, 1)
                dve.tensor_scalar(pen_pad[:, :], vals_all[:, span], PAD_KEY / 2 - 1, MASKED, ALU.is_gt, ALU.mult
                                  ).then_inc(prep_step, 1)
                dve.wait_ge(prep_step, n0 + 2)
                dve.tensor_tensor(pen_all[:, span], pen_all[:, span], pen_pad[:, :], ALU.add
                                  ).then_inc(prep_step, 1)
                dve.wait_ge(prep_step, n0 + 3)
                dve.tensor_scalar(keep_all[:, span], pen_all[:, span], 0.0, None, ALU.is_equal
                                  ).then_inc(prep_step, 1)

            START = 4

            def start_score(g, n0):
                n = n_last[:, bass.ds(g, 1)]
                dve.tensor_scalar(has_last[:, :], n, 0.0, None, ALU.is_gt).then_inc(prep_step, 1)
                dve.wait_ge(prep_step, n0 + 1)
                dve.tensor_scalar(has_pen[:, :], has_last[:, :], -ABSENT, ABSENT, ALU.mult, ALU.add
                                  ).then_inc(prep_step, 1)
                dve.tensor_tensor(last_kept[:, :], last_score[:, bass.ds(g, 1)], has_last[:, :], ALU.mult
                                  ).then_inc(prep_step, 1)
                dve.wait_ge(prep_step, n0 + 3)
                dve.tensor_tensor(last_start[:, bass.ds(g, 1)], last_kept[:, :], has_pen[:, :], ALU.add
                                  ).then_inc(prep_step, 1)

            dve.wait_ge(weights_loaded, 16 * (N_WEIGHT + 4))
            dve.tensor_tensor(w_hist[:, :], w_hist[:, :], w_diff[:, :], ALU.add)
            dve.tensor_scalar(w_item[D:P, :], w_item[D:P, :], -1.0, None, ALU.mult)
            chain(dve.tensor_tensor(w_tmp[:, :], w_item[0:D, 0:D], w_diff_lo[:, :], ALU.subtract))
            dve.scalar_tensor_tensor(out=w_last[:, :], in0=w_prod[0:D, 0:D], scalar=last_col[:, :],
                                     in1=w_tmp[:, :], op0=ALU.mult, op1=ALU.add).then_inc(w_ready, 1)

            PER_GROUP = PREP + 4 + START
            dve.sem_inc(prep_step, 1)
            FIRST = 1
            dve.wait_ge(pool_zeroed, 1)
            dve.wait_ge(hist0_gathered, 16)
            with dve.Fori(0, 1) as z:
                n_first, k_first = load_chunks(dve, z), load_before(dve, z)
                prepare(z, z + FIRST)
                dve.wait_ge(prep_step, z + (FIRST + PREP))
                dve.sem_inc(sorting, 1)
                with dve.Fori(0, n_first) as c:
                    sort_step(k_first + c)

            chain(dve.tensor_copy(sums[0][:, :], slots_of[:, :]))
            shift, k = DEPTH, 0
            while shift < T:
                dve.tensor_copy(sums[1 - k][:, 0:shift], sums[k][:, 0:shift])
                chain(dve.tensor_tensor(sums[1 - k][:, shift:T], sums[k][:, shift:T], sums[k][:, 0:T - shift],
                                        ALU.add))
                shift, k = 2 * shift, 1 - k
            dve.tensor_copy(gathers_to[:, :], sums[k][:, :]).then_inc(slots_ready, 1)
            dve.wait_ge(tables_loaded, 16 * N_TABLE)
            rest = tab
            for k in range(3):
                part = tab_parts[:, :, k * CD:(k + 1) * CD]
                chain(dve.tensor_copy(part, rest[:, :, :]))
                if k < 2:
                    chain(dve.tensor_copy(tab_part[:, :, :], part))
                    chain(dve.tensor_tensor(tab_rest[:, :, :], rest[:, :, :], tab_part[:, :, :], ALU.subtract))
                    rest = tab_rest

            for r in range(G // 4):
                dve.wait_ge(item_kept, r + 1)
                dve.tensor_copy(itemT[D:P, r * N:(r + 1) * N], turned[r][0:D, :]).then_inc(item_low, 1)

            dve.wait_ge(last_l3, G // 4)
            chain(dve.tensor_scalar(last_score[:, 0:G], psS[:, 16:16 + G], b2[:, :], None, ALU.add))
            dve.wait_ge(dense_loaded, 16 * N_DENSE)
            dve.wait_ge(wide_kept, G // 4)

            dve.sem_inc(scores_read, 1)
            dve.sem_inc(pooled, 1)
            dve.sem_inc(dense_step, 1)
            dve.wait_ge(hist_gathered, 16 * (G - 1))

            def times_item(g, t, first=False):
                item = itemT[:, bass.ds(g * P, P)].rearrange("p (o n) -> p o n", o=1).broadcast_to([P, PAIRS, P])
                dve.wait_ge(hT_ready, t + 1)
                if not first:
                    dve.wait_ge(l1_done, t)
                dve.tensor_tensor(pT[:, :].rearrange("p (q n) -> p q n", q=PAIRS),
                                  psT[:, :].rearrange("p (q n) -> p q n", q=PAIRS), item, ALU.mult
                                  ).then_inc(pT_ready, 1)

            def sum_before(t, half, other):
                dve.wait_ge(weighted, t + 1)
                dve.wait_ge(copied, t * 2 + 2 * DEPTH)
                dve.wait_ge(pooled, t + 1)
                dve.tensor_tensor(prod[:, :, :],
                                  rows_x[:, bass.ds(other, 1), :, :].rearrange("p o j f -> p (o j) f"),
                                  e9[:, :].rearrange("p (j o) -> p j o", o=1).broadcast_to([P, SLOTS + 1, AW]),
                                  ALU.mult).then_inc(soft_step, 1)
                dve.wait_ge(soft_step, t * 3 + 1)
                dve.tensor_reduce(rows_x[:, bass.ds(half, 1), SLOTS, :].rearrange("p o f -> p (o f)"),
                                  prod[:, :, :].rearrange("p j f -> p f j"), AX.X, ALU.add).then_inc(pooled, 1)

            def softmax(t):
                flat = bass.ds(t * SLOTS, SLOTS)
                dve.wait_ge(scored, t + 1)
                dve.scalar_tensor_tensor(out=score9[:, 0:SLOTS], in0=psS[:, 0:SLOTS], scalar=b2[:, :],
                                         in1=keep_all[:, flat], op0=ALU.add, op1=ALU.mult
                                         ).then_inc(scores_read, 1)
                dve.wait_ge(scores_read, t + 2)
                dve.tensor_tensor(score9[:, 0:SLOTS], score9[:, 0:SLOTS], pen_all[:, flat], ALU.add
                                  ).then_inc(soft_step, 1)
                dve.wait_ge(soft_step, t * 3 + 3)
                dve.tensor_reduce(neg_max[:, :], score9[:, :], AX.X, ALU.max, negate=True).then_inc(masked, 1)

            def go_on(g, t, half, other):
                sum_before(t, half, other)
                dve.tensor_scalar(score9[:, SLOTS:SLOTS + 1], neg_max[:, :], -1.0, None, ALU.mult
                                  ).then_inc(soft_step, 1)

            def pick_dense(g):
                dve.wait_ge(dense_step, g * 2 + 1)
                dve.tensor_tensor(dense_pick[:, :, :], dense_nat[:, :, :].rearrange("p g f -> p f g"),
                                  is_at[:, bass.ds(g, 1), :].broadcast_to([P, FU + FI, G]), ALU.mult
                                  ).then_inc(dense_step, 1)
                dve.wait_ge(dense_step, g * 2 + 2)
                dve.tensor_reduce(x_all[:, bass.ds(g + 1, 1), X_UD:X_POOL].rearrange("p o f -> p (o f)"),
                                  dense_pick[:, :, :], AX.X, ALU.add).then_inc(dense_step, 1)

            def find_ids(g):
                dve.wait_ge(xT_done, g + 1)
                for k in range(NV + 1):
                    ins = dve.tensor_scalar(hot[:, k, :], wide[:, k // NV, bass.ds(g * P, P)], vocab[:, k:k + 1],
                                            None, ALU.is_equal)
                ins.then_inc(hot_ready, 1)

            def finish(slot, half, t, n0):
                acc = rows_x[:, bass.ds(half, 1), SLOTS, :].rearrange("p o f -> p (o f)")
                dve.wait_ge(pooled, t + 2)
                dve.reciprocal(inv_sum[:, :], acc[:, D:AW]).then_inc(fin_step, 1)
                dve.wait_ge(fin_step, n0 + 1)
                dst = x_all[:, slot, X_POOL:XW] if isinstance(slot, int) else \
                    x_all[:, bass.ds(slot, 1), X_POOL:XW].rearrange("p o f -> p (o f)")
                dve.tensor_scalar(dst, acc[:, 0:D], inv_sum[:, :], None, ALU.mult).then_inc(x_ready, 1)
                return acc

            with dve.Fori(0, 1) as z:
                times_item(z, z, first=True)
            with dve.Fori(0, G) as g:
                before = load_before(dve, g)
                steps = g * PER_GROUP + (FIRST + PREP)
                start = dve.compute_val(dve.snap(before % 2))
                sum_before(before, start, dve.compute_val(dve.snap((before + 1) % 2)))
                acc = finish(g, start, before, g * 2)
                masks(before, steps, load_before(dve, g + 1))
                start_score(g, steps + 4)
                dve.wait_ge(x_ready, g + 1)
                dve.tensor_scalar(acc, last_row[:, :], n_last[:, bass.ds(g, 1)], None, ALU.mult).then_inc(fin_step, 1)
                dve.wait_ge(prep_step, steps + 8)
                dve.tensor_scalar(score9[:, SLOTS:SLOTS + 1], last_start[:, bass.ds(g, 1)], 1.0, None, ALU.mult
                                  ).then_inc(soft_step, 1)
                dve.wait_ge(fin_step, g * 2 + 2)
                times_item(g, before + 1)
                softmax(before)
                t = dve.snap(before + 1)
                half = dve.compute_val(dve.snap(t % 2))
                go_on(g, t, half, dve.compute_val(dve.snap((t + 1) % 2)))
                pick_dense(g)
                next_before = dve.value_load(plan[0:1, bass.ds(g + 33, 1)], min_val=0, max_val=G * MAXC)
                with dve.If(g < G - 1):
                    prepare(g + 1, steps + 8)
                    dve.wait_ge(prep_step, steps + 8 + PREP)
                    dve.sem_inc(sorting, 1)
                    sort_step(next_before + 0)
                with dve.Else():
                    dve.sem_inc(sorted_, 2 * DEPTH)
                times_item(g, t + 1)
                softmax(t)
                with dve.If(g < G - 1):
                    sort_step(next_before + 1)
                find_ids(g)
                last_chunk = load_last(dve, g)
                chunks = dve.snap(last_chunk + 1)
                next_chunks = dve.value_load(plan[0:1, bass.ds(g + 1, 1)], min_val=DUMMY, max_val=MAXC)
                def later_chunk(c, next_g):
                    t = dve.snap(before + c)
                    half = dve.compute_val(dve.snap(t % 2))
                    go_on(g, t, half, dve.compute_val(dve.snap((t + 1) % 2)))
                    with dve.If(c < next_chunks):
                        sort_step(next_before + c)
                    times_item(next_g, t + 1)
                    softmax(t)

                with dve.Fori(2, last_chunk) as c:
                    later_chunk(c, g)
                later_chunk(last_chunk, g + 1)
                with dve.If(chunks < next_chunks):
                    with dve.Fori(chunks, next_chunks) as c:
                        sort_step(next_before + c)
            with dve.Fori(0, 1) as z:
                total = dve.value_load(plan[0:1, bass.ds(z + (32 + G), 1)], min_val=G * MIN_CHUNKS, max_val=G * MAXC)
                half = dve.compute_val(dve.snap(total % 2))
                sum_before(total, half, dve.compute_val(dve.snap((total + 1) % 2)))
                finish(G, half, total, z + G * 2)
            dve.wait_ge(probs_ready, 1)
            chain(dve.tensor_tensor(
                probs_pick[:, :, :], is_at[:, :, :].rearrange("p r g -> p g r"),
                probs[:, :].rearrange("p (o r) -> p o r", o=1).broadcast_to([P, G, G]), ALU.mult))
            dve.tensor_reduce(probs_nat[:, :], probs_pick[:, :, :], AX.X, ALU.add).then_inc(probs_ready, 1)


_NAMES = {
    "user_dense": "r_user_dense", "user_id": "r_user_id", "item_id": "r_item_id",
    "item_category": "r_item_category", "item_dur_bkt": "r_item_dur_bkt", "item_dense": "r_item_dense",
    "history": "r_history_seq",
} | {n: f"L0_rec_{n}" for n in (
    "user_W", "item_W", "cat_W", "dur_W", "hist_W", "aW0", "ab0", "aW1", "ab1", "aW2", "ab2",
    "mW0", "mb0", "mW1", "mb1", "mW2", "mb2")}


def kernel(**inputs):
    import numpy as np
    import concourse.bacc as bacc
    from concourse.bass_utils import run_bass_kernel_spmd

    nc = bacc.Bacc("TRN2", target_bir_lowering=False, num_devices=1)
    arrays = {k: np.ascontiguousarray(inputs[name]) for k, name in _NAMES.items()}
    groups = arrays["history"].shape[0] // P
    arrays["ident"] = np.eye(P, dtype=np.float32)
    arrays["scan"] = np.concatenate(
        [np.eye(groups, dtype=np.float32), np.triu(np.ones((groups, groups + 1), np.float32), 1)], axis=1)
    lanes = np.tile(np.arange(groups + 1, dtype=np.float32), (P, 1))
    lanes[:, groups] = np.arange(P) * groups
    arrays["lanes"] = lanes
    pieces = -(-arrays["cat_W"].shape[0] // P)
    rows = arrays["cat_W"].shape[0] // pieces
    vocab = np.arange(P, dtype=np.float32)[:, None] + np.float32(rows) * np.arange(pieces + 1, dtype=np.float32)
    vocab[:, pieces] = np.arange(P)
    arrays["vocab"] = vocab
    t = groups * -(-arrays["history"].shape[1] // SLOTS) + DEPTH
    arrays["starts"] = np.tile(np.arange(t, dtype=np.float32) * SLOTS, (groups, 1))
    args = {k: nc.dram_tensor(f"in_{k}", v.shape, mybir.dt.from_np(v.dtype), kind="ExternalInput").ap()
            for k, v in arrays.items()}
    out = nc.dram_tensor("out_y", [arrays["history"].shape[0]], F32, kind="ExternalOutput").ap()
    build(nc, args, out)
    r = run_bass_kernel_spmd(nc, [{f"in_{k}": v for k, v in arrays.items()}], core_ids=[0])
    return np.asarray(r.results[0]["out_y"])
```
